# Optimizing a Trainium2 kernel written in Bass

```python
import numpy as np
import jax
import jax.numpy as jnp

def _softmax(x, axis=-1):
    return jax.nn.softmax(x, axis=axis)

def _gelu(x):
    return jax.nn.gelu(x, approximate=True)

def _silu(x):
    return jax.nn.silu(x)

def _sigmoid(x):
    return jax.nn.sigmoid(x)

def _layernorm(x, axis=-1, eps=1e-05):
    m = jnp.mean(x, axis=axis, keepdims=True)
    v = jnp.var(x, axis=axis, keepdims=True)
    return (x - m) / jnp.sqrt(v + eps)

def _scatter_add(tgt, idx, src, axis=0):
    return tgt.at[idx].add(src)

def _segment_sum(src, seg, n):
    return jax.ops.segment_sum(src, seg, n)
kernel_name = 'mk_decoder_postln_d1_seqx_r8_9e42a9'

def setup_inputs(seed: int=0):
    np.random.seed(seed)
    _w = jnp.asarray

    def _rec_inputs():
        import jax
        import jax.numpy as jnp
        _rk = jax.random.key(seed)
        x = -0.0009532 + 1.001 * jax.random.normal(jax.random.fold_in(_rk, 1), (8, 128, 512), jnp.float32)
        _lenS = 128 - jax.random.randint(jax.random.fold_in(_rk, 7), (8,), 0, max(1, 128 // 4) + 1, jnp.int32)
        _lenS2 = 128 - jax.random.randint(jax.random.fold_in(_rk, 8), (8,), 0, max(1, 128 // 4) + 1, jnp.int32)
        _ctx_4096P = jax.random.normal(jax.random.fold_in(_rk, 11), (8, 16, 512), jnp.float32)
        _ctx_4096c = jax.random.dirichlet(jax.random.fold_in(_rk, 511), 0.3 * jnp.ones((16,), jnp.float32), (8, 128))
        _ctx_4096t = jnp.einsum('bsk,bkd->bsd', _ctx_4096c, _ctx_4096P)
        _ctx_4096t = _ctx_4096t * jax.lax.rsqrt(jnp.mean(jnp.square(_ctx_4096t)) + 1e-12) * 0.953939
        ctx_4096 = -0.000394068 + 0.999852 * (_ctx_4096t + 0.3 * jax.random.normal(jax.random.fold_in(_rk, 611), (8, 128, 512), jnp.float32))
        return (x, ctx_4096)
    x, ctx_4096 = _rec_inputs()

    def _L0_attn_setup():
        import jax, jax.numpy as jnp
        import numpy as np
        import math
        B, S, H = (1, 256, 512)
        NH, NKV, HD = (32, 8, 128)
        GS = 128
        WBITS = 4
        ZERO = float(2 ** (WBITS - 1))
        THETA = 10000.0

        def _dequant_matmul(x, qw, scales):
            w = (qw.astype(jnp.float32) - ZERO) * jnp.repeat(scales, GS, axis=0)
            return x @ w

        def _rope_tables(seq_len, dtype):
            inv_freq = 1.0 / THETA ** (jnp.arange(0, HD, 2, dtype=jnp.float32) / HD)
            freqs = jnp.arange(seq_len, dtype=jnp.float32)[:, None] * inv_freq
            emb = jnp.concatenate([freqs, freqs], axis=-1)
            return (jnp.cos(emb).astype(dtype), jnp.sin(emb).astype(dtype))

        def _rotate_half(x):
            x1, x2 = jnp.split(x, 2, axis=-1)
            return jnp.concatenate([-x2, x1], axis=-1)

        def _apply_rope(x, cos, sin):
            return x * cos[None, None] + _rotate_half(x) * sin[None, None]
        key = jax.random.key(seed)
        ks = jax.random.split(key, 9)
        small = lambda k, shp: jax.random.uniform(k, shp, jnp.float32) * 0.01 + 0.001
        return {'hidden_states': jax.random.normal(ks[0], (B, S, H), jnp.float32), 'scales_q': small(ks[1], (H // GS, NH * HD)), 'scales_k': small(ks[2], (H // GS, NKV * HD)), 'scales_v': small(ks[3], (H // GS, NKV * HD)), 'scales_o': small(ks[4], (NH * HD // GS, H)), 'qw_q': jax.random.randint(ks[5], (H, NH * HD), 0, 2 ** WBITS, jnp.int32), 'qw_k': jax.random.randint(ks[6], (H, NKV * HD), 0, 2 ** WBITS, jnp.int32), 'qw_v': jax.random.randint(ks[7], (H, NKV * HD), 0, 2 ** WBITS, jnp.int32), 'qw_o': jax.random.randint(ks[8], (NH * HD, H), 0, 2 ** WBITS, jnp.int32)}
    _L0_attn_all = _L0_attn_setup()
    _L0_attn_in = {k: v for k, v in _L0_attn_all.items() if k in ('scales_q', 'scales_k', 'scales_v', 'scales_o', 'qw_q', 'qw_k', 'qw_v', 'qw_o')}
    del _L0_attn_all

    def _L0_xattn_setup():
        import jax, jax.numpy as jnp
        import numpy as np
        B, S, D = (2, 197, 512)
        HEADS = 16
        key = jax.random.key(seed)
        ks = jax.random.split(key, 9)
        inp = {'q': jax.random.normal(ks[0], (B, S, D), dtype=jnp.float32), 'v': jax.random.normal(ks[1], (B, S, D), dtype=jnp.float32), 'k': jax.random.normal(ks[2], (B, S, D), dtype=jnp.float32), 'Wq': jax.random.normal(ks[3], (D, D), dtype=jnp.float32) * 0.02, 'bq': jax.random.normal(ks[4], (D,), dtype=jnp.float32) * 0.02, 'Wk': jax.random.normal(ks[5], (D, D), dtype=jnp.float32) * 0.02, 'bk': jax.random.normal(ks[6], (D,), dtype=jnp.float32) * 0.02, 'Wv': jax.random.normal(ks[7], (D, D), dtype=jnp.float32) * 0.02, 'bv': jax.random.normal(ks[8], (D,), dtype=jnp.float32) * 0.02, 'head_num': HEADS}
        return inp
    _L0_xattn_all = _L0_xattn_setup()
    _L0_xattn_in = {k: v for k, v in _L0_xattn_all.items() if k in ('Wq', 'bq', 'Wk', 'bk', 'Wv', 'bv')}
    del _L0_xattn_all

    def _L0_ffn_setup():
        import jax, jax.numpy as jnp
        import numpy as np
        B, S, IN, OUT = (4, 256, 512, 512)
        E, K, R = (8, 2, 16)
        CAP_FACTOR = 3.0
        ALPHA = 1.0 / R
        LN_EPS = 1e-05
        key = jax.random.key(seed)
        ks = jax.random.split(key, 6)
        return {'x': jax.random.normal(ks[0], (B, S, IN), dtype=jnp.float32), 'weight': jax.random.normal(ks[1], (OUT, IN), dtype=jnp.float32) * 0.02, 'lora_A': jax.random.normal(ks[2], (E, IN, R), dtype=jnp.float32) / np.sqrt(R), 'lora_B': jax.random.normal(ks[3], (E, R, OUT), dtype=jnp.float32) * 0.02, 'gw1': jax.random.normal(ks[4], (4 * E, IN), dtype=jnp.float32) * 0.02, 'gb1': jnp.zeros((4 * E,), dtype=jnp.float32), 'ln_gamma': jnp.ones((4 * E,), dtype=jnp.float32), 'ln_beta': jnp.zeros((4 * E,), dtype=jnp.float32), 'gw2': jax.random.normal(ks[5], (E, 4 * E), dtype=jnp.float32) * 0.02, 'gb2': jnp.zeros((E,), dtype=jnp.float32)}
    _L0_ffn_all = _L0_ffn_setup()
    _L0_ffn_in = {k: v for k, v in _L0_ffn_all.items() if k in ('weight', 'lora_A', 'lora_B', 'gw1', 'gb1', 'ln_gamma', 'ln_beta', 'gw2', 'gb2')}
    del _L0_ffn_all
    return {'x': x, 'ctx_4096': ctx_4096, 'L0_attn_scales_q': _L0_attn_in['scales_q'], 'L0_attn_scales_k': _L0_attn_in['scales_k'], 'L0_attn_scales_v': _L0_attn_in['scales_v'], 'L0_attn_scales_o': _L0_attn_in['scales_o'], 'L0_attn_qw_q': _L0_attn_in['qw_q'], 'L0_attn_qw_k': _L0_attn_in['qw_k'], 'L0_attn_qw_v': _L0_attn_in['qw_v'], 'L0_attn_qw_o': _L0_attn_in['qw_o'], 'L0_xattn_Wq': _L0_xattn_in['Wq'], 'L0_xattn_bq': _L0_xattn_in['bq'], 'L0_xattn_Wk': _L0_xattn_in['Wk'], 'L0_xattn_bk': _L0_xattn_in['bk'], 'L0_xattn_Wv': _L0_xattn_in['Wv'], 'L0_xattn_bv': _L0_xattn_in['bv'], 'L0_ffn_weight': _L0_ffn_in['weight'], 'L0_ffn_lora_A': _L0_ffn_in['lora_A'], 'L0_ffn_lora_B': _L0_ffn_in['lora_B'], 'L0_ffn_gw1': _L0_ffn_in['gw1'], 'L0_ffn_gb1': _L0_ffn_in['gb1'], 'L0_ffn_ln_gamma': _L0_ffn_in['ln_gamma'], 'L0_ffn_ln_beta': _L0_ffn_in['ln_beta'], 'L0_ffn_gw2': _L0_ffn_in['gw2'], 'L0_ffn_gb2': _L0_ffn_in['gb2']}

def reference(x, ctx_4096, L0_attn_scales_q, L0_attn_scales_k, L0_attn_scales_v, L0_attn_scales_o, L0_attn_qw_q, L0_attn_qw_k, L0_attn_qw_v, L0_attn_qw_o, L0_xattn_Wq, L0_xattn_bq, L0_xattn_Wk, L0_xattn_bk, L0_xattn_Wv, L0_xattn_bv, L0_ffn_weight, L0_ffn_lora_A, L0_ffn_lora_B, L0_ffn_gw1, L0_ffn_gb1, L0_ffn_ln_gamma, L0_ffn_ln_beta, L0_ffn_gw2, L0_ffn_gb2):
    import jax
    import jax.numpy as jnp

    def _L0_attn_ref(hidden_states, scales_q, scales_k, scales_v, scales_o, qw_q, qw_k, qw_v, qw_o):
        import jax, jax.numpy as jnp
        import numpy as np
        import math
        B, S, H = (1, 256, 512)
        NH, NKV, HD = (32, 8, 128)
        GS = 128
        WBITS = 4
        ZERO = float(2 ** (WBITS - 1))
        THETA = 10000.0

        def _dequant_matmul(x, qw, scales):
            w = (qw.astype(jnp.float32) - ZERO) * jnp.repeat(scales, GS, axis=0)
            return x @ w

        def _rope_tables(seq_len, dtype):
            inv_freq = 1.0 / THETA ** (jnp.arange(0, HD, 2, dtype=jnp.float32) / HD)
            freqs = jnp.arange(seq_len, dtype=jnp.float32)[:, None] * inv_freq
            emb = jnp.concatenate([freqs, freqs], axis=-1)
            return (jnp.cos(emb).astype(dtype), jnp.sin(emb).astype(dtype))

        def _rotate_half(x):
            x1, x2 = jnp.split(x, 2, axis=-1)
            return jnp.concatenate([-x2, x1], axis=-1)

        def _apply_rope(x, cos, sin):
            return x * cos[None, None] + _rotate_half(x) * sin[None, None]
        b, s, _ = hidden_states.shape
        q = _dequant_matmul(hidden_states, qw_q, scales_q).reshape(b, s, NH, HD).transpose(0, 2, 1, 3)
        k = _dequant_matmul(hidden_states, qw_k, scales_k).reshape(b, s, NKV, HD).transpose(0, 2, 1, 3)
        v = _dequant_matmul(hidden_states, qw_v, scales_v).reshape(b, s, NKV, HD).transpose(0, 2, 1, 3)
        cos, sin = _rope_tables(s, hidden_states.dtype)
        q = _apply_rope(q, cos, sin)
        k = _apply_rope(k, cos, sin)
        rep = NH // NKV
        k = jnp.repeat(k, rep, axis=1)
        v = jnp.repeat(v, rep, axis=1)
        scores = jnp.einsum('bhqd,bhkd->bhqk', q, k) / math.sqrt(HD)
        causal = jnp.tril(jnp.ones((s, s), dtype=bool))
        scores = jnp.where(causal[None, None], scores, jnp.finfo(scores.dtype).min)
        attn = jax.nn.softmax(scores.astype(jnp.float32), axis=-1).astype(q.dtype)
        ctx = jnp.einsum('bhqk,bhkd->bhqd', attn, v)
        ctx = ctx.transpose(0, 2, 1, 3).reshape(b, s, NH * HD)
        return _dequant_matmul(ctx, qw_o, scales_o)

    def _L0_xattn_ref(q, v, k, Wq, bq, Wk, bk, Wv, bv, head_num):
        import jax, jax.numpy as jnp
        import numpy as np
        B, S, D = (2, 197, 512)
        HEADS = 16
        b, s, _ = q.shape
        hide = Wq.shape[0]
        hd = hide // head_num

        def proj(x, W, bias):
            y = x @ W.T + bias
            return y.reshape(b, s, head_num, hd).transpose(0, 2, 1, 3).reshape(b * head_num, s, hd)
        Q = proj(q, Wq, bq)
        K = proj(k, Wk, bk)
        V = proj(v, Wv, bv)
        scores = jnp.einsum('bqd,bkd->bqk', Q, K) / jnp.sqrt(jnp.asarray(hd, jnp.float32))
        attn = jax.nn.softmax(scores, axis=0)
        res = jnp.einsum('bqk,bkd->bqd', attn, V)
        out = res.reshape(b, head_num, s, hd).transpose(0, 2, 3, 1).reshape(b, s, hd * head_num)
        return out

    def _L0_ffn_ref(x, weight, lora_A, lora_B, gw1, gb1, ln_gamma, ln_beta, gw2, gb2):
        import jax, jax.numpy as jnp
        import numpy as np
        B, S, IN, OUT = (4, 256, 512, 512)
        E, K, R = (8, 2, 16)
        CAP_FACTOR = 3.0
        ALPHA = 1.0 / R
        LN_EPS = 1e-05
        orig_shape = x.shape
        xf = x.reshape(-1, orig_shape[-1])
        N = xf.shape[0]
        capacity = int(CAP_FACTOR * N / E)
        h = xf @ gw1.T + gb1
        mu = jnp.mean(h, axis=-1, keepdims=True)
        var = jnp.mean((h - mu) ** 2, axis=-1, keepdims=True)
        h = (h - mu) * jax.lax.rsqrt(var + LN_EPS) * ln_gamma + ln_beta
        h = jax.nn.relu(h)
        gates = h @ gw2.T + gb2
        top_v, top_i = jax.lax.top_k(gates, K)
        top_g = jax.nn.softmax(top_v, axis=-1)
        onehot = (top_i[..., None] == jnp.arange(E)).astype(xf.dtype)
        counts = onehot.sum(axis=0)
        allowed = (counts <= capacity).astype(xf.dtype)
        w = jnp.einsum('nke,nk,ke->ne', onehot, top_g, allowed)
        main = xf @ weight.T
        tmp = jnp.einsum('ni,eir->enr', xf, lora_A)
        tmp = tmp * w.T[:, :, None]
        lora = jnp.einsum('enr,ero->no', tmp, lora_B) * ALPHA
        out = main + lora
        return out.reshape(*orig_shape[:-1], weight.shape[0])
    x = _layernorm(x + _L0_attn_ref(x, L0_attn_scales_q, L0_attn_scales_k, L0_attn_scales_v, L0_attn_scales_o, L0_attn_qw_q, L0_attn_qw_k, L0_attn_qw_v, L0_attn_qw_o), axis=-1)
    x = _layernorm(x + _L0_xattn_ref(x, ctx_4096, ctx_4096, L0_xattn_Wq, L0_xattn_bq, L0_xattn_Wk, L0_xattn_bk, L0_xattn_Wv, L0_xattn_bv, 16), axis=-1)
    x = _layernorm(x + _L0_ffn_ref(x, L0_ffn_weight, L0_ffn_lora_A, L0_ffn_lora_B, L0_ffn_gw1, L0_ffn_gb1, L0_ffn_ln_gamma, L0_ffn_ln_beta, L0_ffn_gw2, L0_ffn_gb2), axis=-1)
    return x

_drawn_inputs = setup_inputs


def setup_inputs(seed=0):
    import zlib

    import numpy as np

    out = dict(_drawn_inputs(seed))
    spreads = {'L0_ffn_gb1': (0.0, 0.8),
     'L0_ffn_ln_gamma': (1.0, 0.6),
     'L0_ffn_ln_beta': (0.0, 0.8),
     'L0_ffn_gb2': (0.0, 0.472)}
    factors = {'L0_xattn_bq': 8.0,
     'L0_xattn_bk': 8.0,
     'L0_xattn_bv': 3.137,
     'L0_ffn_lora_A': 4.85,
     'L0_ffn_lora_B': 4.846,
     'L0_ffn_gw1': 5.479,
     'L0_ffn_gw2': 5.433}
    for name, (base, spread) in spreads.items():
        noise = np.random.default_rng([zlib.crc32(name.encode()), seed]).standard_normal(out[name].shape)
        drawn = base * np.exp(spread * noise) if base else spread * noise
        out[name] = jnp.asarray(drawn.astype(out[name].dtype))
    for name, factor in factors.items():
        out[name] = (out[name] * factor).astype(out[name].dtype)
    return out
```

```python
from contextlib import ExitStack

import numpy as np

import concourse.bass as bass
from concourse import mybir

F32 = mybir.dt.float32
F32R = mybir.dt.float32r
BF16 = mybir.dt.bfloat16
I32 = mybir.dt.int32
U32 = mybir.dt.uint32
ALU = mybir.AluOpType
ACT = mybir.ActivationFunctionType
AX = mybir.AxisListType

P = 128
NB = 8
T = NB * P
D = 512
KC = D // P
NKV = 8
QPK = 4
NT = 2 + QPK
HALF = T // 2
BPH = NB // 2
ZERO = 8.0
SCALE = 1.0 / float(np.sqrt(P))
NEG = -3.0e38

XH = 16
XD = D // XH
XSCALE = 1.0 / float(np.sqrt(XD))
E = 8
R = 16
ER = E * R
GH = 4 * E
CAPACITY = float(int(3.0 * T / E))
ALPHA = 1.0 / R
EPS = 1e-5

LN_GROUPS = [[(0, 4), (4, 4)], [(0, 4), (4, 4)], [(0, 2), (2, 2), (4, 2), (6, 2)]]
ROPE_TILES = [0, 2, 3, 4, 5]
ARENA = 34816


def wait(eng, sem, value):
    if isinstance(value, int) and value <= 0:
        return
    eng.wait_ge(sem, value)


def build(nc, t, out):
    with ExitStack() as ctx:
        def sb(name, shape, dt=F32):
            return ctx.enter_context(nc.sbuf_tensor(name, shape, dt))

        def sem(name):
            return ctx.enter_context(nc.semaphore(name))

        x_hi = sb("x_hi", [P, KC, T], F32R)
        x_lo = sb("x_lo", [P, KC, T], F32R)
        w_sb = sb("w_sb", [P, NT, KC, P], F32R)
        y = sb("y", [P, NB, D])
        consts = sb("consts", [P, 4, P])
        ident = consts[:, 0, :]
        ident_b = sb("ident_b", [P, P], BF16)
        mask_b = sb("mask_b", [P, QPK, P], BF16)
        small = sb("small", [P, 512])
        arena = sb("arena", [P, ARENA])

        at = [0]

        def carve(*shape, base=None):
            n = int(np.prod(shape))
            if base is not None:
                at[0] = base
            a = at[0]
            at[0] += n
            assert at[0] <= ARENA, at[0]
            v = arena[:, a:a + n]
            if len(shape) == 2:
                return v.rearrange("p (a b) -> p a b", b=shape[1])
            if len(shape) == 3:
                return v.rearrange("p (a b c) -> p a b c", b=shape[1], c=shape[2])
            return v

        w_int = carve(NT * KC * P).bitcast(I32).rearrange("p (c g n) -> p c g n", c=NT, g=KC)
        wo = carve(2, QPK, D)
        wo_int = carve(QPK * D).bitcast(I32).rearrange("p (h n) -> p h n", h=QPK)
        wo_scale = carve(QPK, D)
        q_t = carve(QPK, T)
        k_t = carve(T)
        v_sb = carve(NB, P)
        sum_a = carve(2, HALF)
        sum_b = carve(2, HALF)
        raw = carve(2, HALF)
        turned = carve(2, HALF)
        raw_cos = carve(2, HALF)
        v_t = carve(HALF)
        probs = carve(2, QPK, P)
        probs_t = carve(2, QPK, P)
        heads_t = carve(2, QPK, P)
        scales = carve(NKV * NT * KC)

        def scale_of(j, c, g):
            return scales[:, bass.ds((NT * KC) * j + (KC * c + g), 1)]

        def wo_of(par, h):
            return wo[:, bass.ds(par, 1), h, :].rearrange("p a n -> p (a n)")

        cos = consts[:, 2, :]
        sin = consts[:, 3, :]

        def by_tile(v):
            return v.rearrange("p (b q) -> p b q", q=P)

        def every_tile(v):
            return v.unsqueeze(1).broadcast_to([P, BPH, P])

        x_stage = q_t

        row_max = small[:, 0:8].rearrange("p (s h) -> p s h", s=2)
        neg_max = small[:, 8:16].rearrange("p (s h) -> p s h", s=2)
        row_sum = small[:, 16:24].rearrange("p (s h) -> p s h", s=2)
        row_inv = small[:, 24:32].rearrange("p (s h) -> p s h", s=2)

        xs = carve(NB, 16 * P, base=0)
        wk2 = carve(KC, D, base=0)
        wq2 = carve(KC, D, base=3072)
        x2_t = carve(KC, T, base=5120)
        q2_t = carve(KC, T, base=16384)
        k2_t = carve(KC, T)
        v2 = carve(NB, D)
        ctx_t = carve(KC, T)
        wv2 = carve(KC, D)
        x_max = v2.rearrange("p a b -> p (a b)")[:, 0:2048]
        x_sum = q2_t.rearrange("p a b -> p (a b)")[:, 0:2048]
        x_m = small[:, 128:256]
        x_r = small[:, 256:384]

        x3_t = carve(KC, T, base=16384)
        gate_tmp = carve(P * NB, base=20480)
        tmp = gate_tmp.rearrange("p (b er) -> p b er", b=NB)
        tmp_t = carve(T)
        hid_t = carve(T)
        hid = carve(NB, GH)
        hid_sq = carve(NB, GH)
        gates = carve(NB, E)
        top_v = carve(NB, E)
        top_i = carve(NB * E).bitcast(U32).rearrange("p (b e) -> p b e", e=E)
        top_f = carve(NB, 2)
        onehot = carve(NB, 2 * E)
        gated = carve(NB, 2 * E)
        w_exp = carve(NB, E)
        allowed = carve(2 * E)
        g_mean = carve(NB)
        g_var = carve(NB)
        g_rstd = carve(NB)
        g_diff = carve(NB)
        g_e2 = carve(NB)
        g_den = carve(NB)
        g_top = carve(NB, 2)
        w_main = carve(KC, D, base=28672)
        w_a = carve(KC, ER)
        w_g1 = carve(KC, GH)
        w_b = carve(D)

        params = sb("params", [P, 3 * GH + E + E])
        gb1_b = params[:, 0:GH]
        gamma_b = params[:, GH:2 * GH]
        beta_b = params[:, 2 * GH:3 * GH]
        gb2_b = params[:, 3 * GH:3 * GH + E]
        numbers = params[:, 3 * GH + E:3 * GH + 2 * E]
        gw2_t = sb("gw2_t", [GH, E])
        bias_qk = sb("bias_qk", [P, 2 * KC])
        bias_v = sb("bias_v", [1, D])
        ones = sb("ones", [P, P])
        minus_half = sb("minus_half", [P, NB])
        stats = sb("stats", [P, NB, 6])
        mean_var = sb("mean_var", [P, NB, 2])
        var_eps = sb("var_eps", [P, NB])
        rstd = sb("rstd", [P, NB])

        ps = ctx.enter_context(nc.psum_tensor("ps", [P, 8, 512], F32))
        banks = [ps[:, i, :] for i in range(8)]
        proj_ps = banks[0:3]
        score_ps = banks[3:5]
        turn_ps = banks[5]
        pv_ps = banks[6]
        out_ps = banks[7]

        consts_in = sem("consts_in")
        x_in = [sem("x_first_half_in"), sem("x_second_half_in")]
        w_first_in = [sem(f"w_first_{c}_in") for c in range(NT)]
        y_in = sem("y_in")
        scales_in = sem("scales_in")
        w_in = sem("w_in")
        wo_first_in = sem("wo_first_in")
        wo_in = sem("wo_in")
        mask_ready = sem("mask_ready")
        x_hi_ready = sem("x_hi_ready")
        x_lo_ready = sem("x_lo_ready")
        w_ready = sem("w_ready")
        wo_ready = sem("wo_ready")
        unit_done = sem("unit_done")
        act_scaled = sem("act_scaled")
        dve_scaled = sem("dve_scaled")
        tile_summed = sem("tile_summed")
        turned_in = [sem("turned_even_in"), sem("turned_odd_in")]
        cos_done = sem("cos_done")
        sin_done = sem("sin_done")
        rotated = sem("rotated")
        v_turned = sem("v_turned")
        v_ready = sem("v_ready")
        scored = sem("scored")
        max_done = sem("max_done")
        neg_ready = sem("neg_ready")
        exp_done = sem("exp_done")
        inv_ready = sem("inv_ready")
        probs_ready = sem("probs_ready")
        probs_turned = sem("probs_turned")
        probs_t_ready = sem("probs_t_ready")
        pv_done = sem("pv_done")
        heads_ready = sem("heads_ready")
        out_done = sem("out_done")
        y_added = sem("y_added")
        stored = sem("stored")
        k2_in = sem("k2_in")
        q2_in = sem("q2_in")
        v2_in = sem("v2_in")
        params_in = sem("params_in")
        experts_in = sem("experts_in")
        ones_ready = sem("ones_ready")
        stats_done = sem("stats_done")
        tile_stats = sem("tile_stats")
        eps_added = sem("eps_added")
        rstd_ready = sem("rstd_ready")
        normed = sem("normed")
        x_turned = sem("x_turned")
        x_t_ready = sem("x_t_ready")
        proj2_done = sem("proj2_done")
        proj2_copied = sem("proj2_copied")
        scored2 = sem("scored2")
        scores2_copied = sem("scores2_copied")
        scores2_maxed = sem("scores2_maxed")
        max2_ready = sem("max2_ready")
        shifted2 = sem("shifted2")
        exp2_done = sem("exp2_done")
        summed2 = sem("summed2")
        sum2_folded = sem("sum2_folded")
        weights2_ready = sem("weights2_ready")
        pv2_done = sem("pv2_done")
        attended2 = sem("attended2")
        hidden_done = sem("hidden_done")
        lora_a_done = sem("lora_a_done")
        main_done = sem("main_done")
        main_added = sem("main_added")
        gate_step = sem("gate_step")
        gate_var = sem("gate_var")
        gate_rstd = sem("gate_rstd")
        hid_ready = sem("hid_ready")
        hid_turned = sem("hid_turned")
        hid_t_ready = sem("hid_t_ready")
        gates_done = sem("gates_done")
        onehot_ready = sem("onehot_ready")
        counted = sem("counted")
        diff_ready = sem("diff_ready")
        e2_ready = sem("e2_ready")
        tmp_ready = sem("tmp_ready")
        tmp_turned = sem("tmp_turned")
        tmp_t_ready = sem("tmp_t_ready")
        lora_done = sem("lora_done")
        lora_added = sem("lora_added")

        block = ctx.enter_context(nc.Block())

        UNITS = NT * KC
        RT = len(ROPE_TILES)

        def turned_count(p, c):
            return 32 * (3 * p + c // 2 + 1) if c % 2 == 0 else 32 * (2 * p + (c - 3) // 2 + 1)

        def slot_rotated(p, c):
            before = {0: (-1, 3), 2: (0, 0), 4: (0, 1), 3: (-1, 4), 5: (0, 2)}[c]
            return RT * (p + before[0]) + before[1] + 1

        @block.sync
        def _(sp):
            def load_x(half):
                for g in range(KC):
                    sp.dma_start(x_stage[:, g, half * HALF:(half + 1) * HALF],
                                 t["x_t"][:, g, half * HALF:(half + 1) * HALF]).then_inc(x_in[half], 16)

            load_x(0)
            sp.dma_start(w_int[:, 0], t["qkv"][0][:, 0]).then_inc(w_first_in[0], 16)
            sp.dma_start(scales[:, :], t["qkv_scales"]).then_inc(scales_in, 16)
            for c in range(1, NT):
                sp.dma_start(w_int[:, c], t["qkv"][0][:, c]).then_inc(w_first_in[c], 16)
                if c == 1:
                    sp.dma_start(consts[:, :, :], t["consts"]).then_inc(consts_in, 16)
            load_x(1)

            def load_wo(j):
                wait(sp, wo_ready, QPK * j)
                sp.dma_start(wo_int[:, :, :], t["o"][j]).then_inc(wo_in, 16)
                sp.dma_start(wo_scale[:, :, :], t["o_scales"][j].partition_broadcast(P)).then_inc(wo_in, 16)

            def load_w(j):
                wait(sp, w_ready, NT * j)
                sp.dma_start(w_int[:, :, :, :], t["qkv"][j]).then_inc(w_in, 16)

            def turn(p, c):
                wait(sp, tile_summed, NT * p + c + 1)
                s = c % 2
                for a, b in ((0, 64), (64, 0)):
                    sp.dma_start(turned[a:a + 64, s, :], raw[b:b + 64, s, :]).then_inc(turned_in[s], 16)

            def turns(p):
                for c in ROPE_TILES:
                    turn(p, c)

            for h, c in enumerate(ROPE_TILES):
                if h < QPK:
                    sp.dma_start(wo_int[:, h, :], t["o"][0][:, h, :]).then_inc(wo_first_in, 16)
                turn(0, c)
                if h < QPK:
                    sp.dma_start(wo_scale[:, h, :], t["o_scales"][0][h].partition_broadcast(P)).then_inc(wo_first_in, 16)
            sp.dma_start(y[:, :, :], t["x"]).then_inc(y_in, 16)
            sp.dma_start(bias_qk[:, :], t["bias_qk"]).then_inc(params_in, 16)
            sp.dma_start(bias_v[:, :], t["bias_v"]).then_inc(params_in, 16)
            sp.dma_start(gw2_t[:, :], t["gw2_t"]).then_inc(params_in, 16)
            sp.dma_start(params[:, :], t["params"].partition_broadcast(P)).then_inc(params_in, 16)

            def iteration(j, last_w):
                load_wo(j + 1)
                turns(2 * j + 1)
                if not last_w:
                    load_w(j + 2)
                turns(2 * j + 2)

            load_w(1)
            load_wo(1)
            for g, c in enumerate(ROPE_TILES):
                turn(1, c)
                if g < KC:
                    sp.dma_start(ctx_t[:, g, :], t["ctx_t"][:, g, :]).then_inc(v2_in, 16)
            load_w(2)
            for g, c in enumerate(ROPE_TILES):
                turn(2, c)
                if g < KC:
                    sp.dma_start(wv2[:, g, :], t["wv2"][:, g, :]).then_inc(v2_in, 16)
            with sp.Fori(1, NKV - 2) as j:
                iteration(j, False)
            iteration(NKV - 2, True)
            turns(2 * NKV - 1)
            sp.wait_ge(w_ready, NT * NKV)
            sp.dma_start(wk2[:, :, :], t["wk2"]).then_inc(k2_in, 16)
            sp.wait_ge(wo_ready, QPK * NKV)
            sp.dma_start(wq2[:, :, :], t["wq2"]).then_inc(q2_in, 16)
            sp.wait_ge(proj2_done, 24)
            sp.dma_start(w_main[:, :, :], t["w_main"]).then_inc(experts_in, 16)
            sp.dma_start(w_a[:, :, :], t["w_a"]).then_inc(experts_in, 16)
            sp.dma_start(w_g1[:, :, :], t["w_g1"]).then_inc(experts_in, 16)
            sp.dma_start(w_b[:, :], t["w_b"]).then_inc(experts_in, 16)
            for b in range(NB):
                sp.wait_ge(normed, 2 * NB + b + 1)
                sp.dma_start(out[:, b, :], y[:, b, :]).then_inc(stored, 16)
            sp.wait_ge(stored, 16 * NB)

        @block.gpsimd
        def _(pool):
            def convert(c):
                nc.gpsimd.tensor_scalar(w_sb[:, c], w_int[:, c], -ZERO, 1.0, ALU.add, ALU.mult).then_inc(w_ready, 1)

            def finish(p, c):
                s = c % 2
                wait(pool, dve_scaled, 2 * (NT * p + c + 1))
                if c == 1:
                    wait(pool, v_turned, p)
                    dst = v_t
                else:
                    wait(pool, rotated, slot_rotated(p, c))
                    dst = raw[:, s, :]
                nc.gpsimd.tensor_tensor(dst, sum_a[:, s, :], sum_b[:, s, :], ALU.add).then_inc(tile_summed, 1)
                if c != 1:
                    wait(pool, tile_summed, NT * p + c + 1)
                    nc.gpsimd.tensor_tensor(by_tile(raw_cos[:, s, :]), by_tile(dst), every_tile(cos), ALU.mult).then_inc(cos_done, 1)

            for c in range(NT):
                wait(pool, w_first_in[c], 16)
                convert(c)
            pool.wait_ge(consts_in, 16)
            for c in range(NT):
                finish(0, c)

            def iteration(j, more):
                if more:
                    wait(pool, w_in, 16 * (j + 1))
                for c in range(NT):
                    finish(2 * j + 1, c)
                    if more:
                        convert(c)
                if more:
                    for c in range(NT):
                        finish(2 * j + 2, c)

            iteration(0, True)
            with pool.Fori(1, NKV - 1) as j:
                iteration(j, True)
            iteration(NKV - 1, False)

            nc.gpsimd.memset(minus_half[:, :], -0.5).then_inc(ones_ready, 1)
            nc.gpsimd.memset(ones[:, :], 1.0).then_inc(ones_ready, 1)
            pool.wait_ge(ones_ready, 2)
            groups = 0

            def inverse_deviation(layer, first, count):
                nonlocal groups
                groups += 1
                pool.wait_ge(tile_stats, layer * NB + first + count)
                nc.gpsimd.tensor_scalar(var_eps[:, first:first + count], mean_var[:, first:first + count, 1], EPS, 1.0,
                                        ALU.add, ALU.mult).then_inc(eps_added, 1)
                pool.wait_ge(eps_added, groups)
                nc.gpsimd.tensor_tensor(rstd[:, first:first + count], var_eps[:, first:first + count],
                                        minus_half[:, 0:count], ALU.pow).then_inc(rstd_ready, 1)

            for first, count in LN_GROUPS[0]:
                inverse_deviation(0, first, count)
            for first, count in LN_GROUPS[1]:
                inverse_deviation(1, first, count)
            pool.wait_ge(gate_var, 1)
            nc.gpsimd.tensor_tensor(g_rstd, g_var, minus_half[:, :], ALU.pow).then_inc(gate_rstd, 1)
            for first, count in LN_GROUPS[2]:
                inverse_deviation(2, first, count)

        @block.scalar
        def _(act):
            def cut_x(half):
                act.wait_ge(x_in[half], 16 * KC)
                for g in range(KC):
                    nc.scalar.activation(x_hi[:, g, half * HALF:(half + 1) * HALF],
                                         x_stage[:, g, half * HALF:(half + 1) * HALF], ACT.Copy).then_inc(x_hi_ready, 1)

            cut_x(0)
            act.wait_ge(scales_in, 16)

            def scale_group(j, p, c, g):
                unit = UNITS * p + KC * c + g
                wait(act, unit_done, unit + 1)
                wait(act, tile_summed, NT * p + c - 1)
                dst = (sum_a if g == 0 else sum_b)[:, c % 2, :]
                nc.scalar.activation(dst, proj_ps[(KC * c + g) % 3][:, :], ACT.Copy,
                                     scale=scale_of(j, c, g)).then_inc(act_scaled, 1)

            def exps(n, b):
                s = b % 2
                wait(act, neg_ready, n + 1)
                wait(act, probs_turned, n - 1)
                for h in range(QPK):
                    last = nc.scalar.activation(probs[:, s, h, :], score_ps[s][:, h * P:(h + 1) * P], ACT.Exp,
                                                bias=neg_max[:, s, h:h + 1], scale=SCALE,
                                                accum_out=row_sum[:, s, h:h + 1])
                last.then_inc(exp_done, 1)

            def copy_probs(n, b):
                s = b % 2
                wait(act, probs_turned, n + 1)
                wait(act, pv_done, n - 1)
                nc.scalar.activation(probs_t[:, s, :, :].rearrange("p h q -> p (h q)"), turn_ps[:, :],
                                     ACT.Copy).then_inc(probs_t_ready, 1)

            def copy_heads(n, b):
                s = b % 2
                wait(act, pv_done, n + 1)
                wait(act, out_done, n - 1)
                nc.scalar.activation(heads_t[:, s, :, :].rearrange("p h q -> p (h q)"), pv_ps[:, :],
                                     ACT.Copy).then_inc(heads_ready, 1)

            def copy_v(p, half):
                wait(act, v_turned, p + 1)
                nc.scalar.activation(v_sb[:, half * BPH:(half + 1) * BPH, :].rearrange("p b d -> p (b d)"),
                                     turn_ps[:, :], ACT.Copy).then_inc(v_ready, 1)

            def phase(j, half, project):
                p = 2 * j + half + 1
                jp = j + half
                for s in range(BPH):
                    b = half * BPH + s
                    n = NB * j + b
                    nxt = (b + 1) % NB
                    if s < 3:
                        if project:
                            if s == 2:
                                copy_v(p, 1 - half)
                            scale_group(jp, p, 2 * s, 0)
                        if s == 0:
                            copy_probs(n, b)
                            if project:
                                scale_group(jp, p, 0, 2)
                            exps(n + 1, nxt)
                        else:
                            exps(n + 1, nxt)
                            copy_probs(n, b)
                            if project:
                                scale_group(jp, p, 2 * s, 2)
                        if project and s == 2:
                            scale_group(jp, p, 5, 0)
                            scale_group(jp, p, 5, 2)
                        copy_heads(n, b)
                        if project and s < 2:
                            for g in (0, 2):
                                scale_group(jp, p, 2 * s + 1, g)
                    else:
                        copy_probs(n, b)
                        copy_heads(n, b)
                        if project:
                            exps(n + 1, nxt)

            for c in range(NT):
                for g in (0, 2):
                    scale_group(0, 0, c, g)
                if c == 2:
                    cut_x(1)
            copy_v(0, 0)
            exps(0, 0)
            phase(0, 0, True)
            phase(0, 1, True)
            with act.Fori(1, NKV - 1) as j:
                phase(j, 0, True)
                phase(j, 1, True)
            phase(NKV - 1, 0, True)
            phase(NKV - 1, 1, False)
            act.wait_ge(params_in, 64)

            def copy_proj2(i, dst, bias=None):
                act.wait_ge(proj2_done, i + 1)
                if bias is None:
                    ins = nc.scalar.activation(dst, banks[i % 3], ACT.Copy)
                else:
                    ins = nc.scalar.activation(dst, banks[i % 3], ACT.Identity, bias=bias)
                ins.then_inc(proj2_copied, 1)

            def copy_x_t(layer, b, dst):
                act.wait_ge(x_turned, layer * NB + b + 1)
                nc.scalar.activation(dst[:, :, b * P:(b + 1) * P],
                                     banks[5 + b % 2].rearrange("p (c q) -> p c q", c=KC), ACT.Copy).then_inc(x_t_ready, 1)

            act.wait_ge(y_added, NKV * NB)
            for i in range(8):
                copy_proj2(i, k2_t[:, i // 2, (i % 2) * HALF:(i % 2 + 1) * HALF], bias_qk[:, 4 + i // 2:5 + i // 2])
            for b in range(NB):
                copy_x_t(0, b, x2_t)
            for i in range(8):
                copy_proj2(8 + i, q2_t[:, i // 2, (i % 2) * HALF:(i % 2 + 1) * HALF], bias_qk[:, i // 2:i // 2 + 1])
            for b in range(NB):
                act.wait_ge(scored2, b + 1)
                nc.scalar.activation(xs[:, b, :], ps[:, 4 * (b % 2):4 * (b % 2) + 4, :].rearrange("p a n -> p (a n)"),
                                     ACT.Copy).then_inc(scores2_copied, 1)
            act.wait_ge(max2_ready, 1)
            for b in range(NB):
                act.wait_ge(shifted2, b + 1)
                nc.scalar.activation(xs[:, b, :], xs[:, b, :], ACT.Exp, scale=XSCALE).then_inc(exp2_done, 1)
                copy_proj2(16 + b, v2[:, b, :])
            for b in range(NB):
                copy_x_t(1, b, x3_t)
            for k in range(2):
                act.wait_ge(hid_turned, 1)
                nc.scalar.activation(hid_t[0:GH, k * 512:(k + 1) * 512], banks[6 + k][0:GH, :], ACT.Copy).then_inc(hid_t_ready, 1)
            act.wait_ge(diff_ready, 1)
            nc.scalar.activation(g_e2, g_diff, ACT.Exp).then_inc(e2_ready, 1)
            for k in range(2):
                act.wait_ge(tmp_turned, 1)
                nc.scalar.activation(tmp_t[:, k * 512:(k + 1) * 512], banks[6 + k], ACT.Copy).then_inc(tmp_t_ready, 1)

        @block.vector
        def _(dve):
            def cut_x(half):
                part = slice(half * HALF, (half + 1) * HALF)
                for g in range(KC):
                    dve.wait_ge(x_hi_ready, KC * half + g + 1)
                    nc.vector.tensor_tensor(x_lo[:, g, part], x_stage[:, g, part], x_hi[:, g, part].bitcast(F32),
                                            ALU.subtract).then_inc(x_lo_ready, 1)

            cut_x(0)
            dve.wait_ge(consts_in, 16)
            nc.vector.tensor_copy(ident_b[:, :], ident).then_inc(mask_ready, 1)
            for h in range(QPK):
                nc.vector.tensor_copy(mask_b[:, h, :], consts[:, 1, :]).then_inc(mask_ready, 1)
            dve.wait_ge(scales_in, 16)

            def add_group(j, p, c, g):
                unit = UNITS * p + KC * c + g
                wait(dve, unit_done, unit + 1)
                wait(dve, act_scaled, 2 * (NT * p + c) + (g + 1) // 2)
                acc = (sum_a if g == 1 else sum_b)[:, c % 2, :]
                nc.vector.scalar_tensor_tensor(acc, proj_ps[(KC * c + g) % 3][:, :],
                                               scale_of(j, c, g), acc,
                                               ALU.mult, ALU.add).then_inc(dve_scaled, 1)

            def rotate(p, c, half):
                s, r = c % 2, ROPE_TILES.index(c)
                wait(dve, turned_in[s], turned_count(p, c))
                nc.vector.tensor_tensor(by_tile(turned[:, s, :]), by_tile(turned[:, s, :]), every_tile(sin),
                                        ALU.mult).then_inc(sin_done, 1)
                wait(dve, sin_done, RT * p + r + 1)
                wait(dve, cos_done, RT * p + r + 1)
                dst = (k_t if c == 0 else q_t[:, c - 2, :])[:, half * HALF:(half + 1) * HALF]
                nc.vector.tensor_tensor(dst, raw_cos[:, s, :], turned[:, s, :], ALU.add).then_inc(rotated, 1)

            def maxima(n, b):
                s = b % 2
                wait(dve, scored, n + 1)
                wait(dve, neg_ready, n - 1)
                nc.vector.tensor_reduce(row_max[:, s, :], score_ps[s][:, :].rearrange("p (h k) -> p h k", k=P),
                                        AX.X, ALU.max).then_inc(max_done, 1)
                wait(dve, max_done, n + 1)
                wait(dve, exp_done, n - 1)
                nc.vector.tensor_scalar(neg_max[:, s, :], row_max[:, s, :], -SCALE, None,
                                        ALU.mult).then_inc(neg_ready, 1)

            def normalise(n, b):
                s = b % 2
                wait(dve, exp_done, n + 1)
                wait(dve, probs_ready, n - 1)
                nc.vector.reciprocal(row_inv[:, s, :], row_sum[:, s, :]).then_inc(inv_ready, 1)
                wait(dve, inv_ready, n + 1)
                nc.vector.tensor_tensor(probs[:, s, :, :], probs[:, s, :, :],
                                        row_inv[:, s, :].unsqueeze(2).broadcast_to([P, QPK, P]), ALU.mult).then_inc(probs_ready, 1)

            def add_out(n, b):
                wait(dve, out_done, n + 1)
                wait(dve, y_added, n - NB + 1)
                nc.vector.tensor_tensor(y[:, b, :], out_ps[:, :], y[:, b, :], ALU.add).then_inc(y_added, 1)

            def convert_wo(j, par, h):
                wait(dve, wo_in, 32 * j)
                wait(dve, out_done, NB * (j - 1))
                nc.vector.scalar_tensor_tensor(wo_of(par, h), wo_int[:, h, :], -ZERO, wo_scale[:, h, :],
                                               ALU.add, ALU.mult).then_inc(wo_ready, 1)

            def phase(j, par, half, project):
                p = 2 * j + half + 1
                jp = j + half
                for s in range(BPH):
                    b = half * BPH + s
                    n = NB * j + b
                    nxt = (b + 1) % NB
                    if s < 3:
                        maxima(n + 1, nxt)
                        if project:
                            add_group(jp, p, 2 * s, 1)
                            if s > 0:
                                rotate(p, 2 * s - 2, 1 - half)
                            add_group(jp, p, 2 * s, 3)
                        normalise(n + 1, nxt)
                        if project:
                            add_group(jp, p, 2 * s + 1, 1)
                            if s == 2:
                                rotate(p, 3, 1 - half)
                            add_group(jp, p, 2 * s + 1, 3)
                        if not (isinstance(j, int) and j == 0 and b == 0):
                            add_out(n - 1, (b - 1) % NB)
                    else:
                        if project:
                            rotate(p, 4, 1 - half)
                        if convert_next(j):
                            for h in (2 * half, 2 * half + 1):
                                convert_wo(j + 1, par, h)
                        if project:
                            rotate(p, 5, 1 - half)
                        add_out(n - 1, b - 1)
                        if project:
                            maxima(n + 1, nxt)
                            normalise(n + 1, nxt)

            def convert_next(j):
                return not (isinstance(j, int) and j == NKV - 1)

            for c in range(NT):
                if c > 1 and c - 2 in ROPE_TILES:
                    rotate(0, c - 2, 0)
                for g in (1, 3):
                    add_group(0, 0, c, g)
                if c == 2:
                    cut_x(1)
            rotate(0, 4, 0)
            rotate(0, 5, 0)
            dve.wait_ge(wo_first_in, 32 * QPK)
            for h in range(QPK):
                convert_wo(0, 0, h)
            maxima(0, 0)
            normalise(0, 0)
            dve.wait_ge(y_in, 16)
            phase(0, 1, 0, True)
            phase(0, 1, 1, True)
            with dve.Fori(1, NKV - 1) as j:
                par = dve.snap((j + 1) % 2)
                phase(j, par, 0, True)
                phase(j, par, 1, True)
            phase(NKV - 1, 0, 0, True)
            phase(NKV - 1, 0, 1, False)
            add_out(NKV * NB - 1, NB - 1)
            rstds = 0

            def layernorm_stats(layer, first, count, after=None, value=0):
                for b in range(first, first + count):
                    if after is not None:
                        dve.wait_ge(after, value + b + 1)
                    nc.vector.bn_stats(stats[:, b, :], y[:, b, :]).then_inc(stats_done, 1)
                dve.wait_ge(rstd_ready, rstds)
                for b in range(first, first + count):
                    dve.wait_ge(stats_done, layer * NB + b + 1)
                    nc.vector.bn_aggr(mean_var[:, b, :], stats[:, b, :]).then_inc(tile_stats, 1)

            def layernorm_apply(layer, first, count):
                nonlocal rstds
                rstds += 1
                dve.wait_ge(rstd_ready, rstds)
                dve.wait_ge(tile_stats, layer * NB + first + count)
                for b in range(first, first + count):
                    nc.vector.tensor_scalar(y[:, b, :], y[:, b, :], mean_var[:, b, 0:1], rstd[:, b:b + 1],
                                            ALU.subtract, ALU.mult).then_inc(normed, 1)

            for first, count in LN_GROUPS[0]:
                layernorm_stats(0, first, count, y_added, (NKV - 1) * NB)
                layernorm_apply(0, first, count)

            for b in range(NB):
                if b > 0:
                    dve.wait_ge(scores2_copied, b + 1)
                    wait(dve, scores2_maxed, b - 1)
                    nc.vector.tensor_tensor(x_max, xs[:, b, :], xs[:, 0, :] if b == 1 else x_max,
                                            ALU.max).then_inc(scores2_maxed, 1)
            dve.wait_ge(scores2_maxed, NB - 1)
            nc.vector.tensor_reduce(x_m, x_max.rearrange("p (g q) -> p q g", q=P), AX.X, ALU.max).then_inc(max2_ready, 1)
            dve.wait_ge(max2_ready, 1)

            def over_groups(v):
                return v.unsqueeze(1).broadcast_to([P, 16, P])

            def by_group(v):
                return v.rearrange("p (g q) -> p g q", q=P)

            def shift(b):
                dve.wait_ge(scores2_copied, b + 1)
                nc.vector.tensor_tensor(by_group(xs[:, b, :]), by_group(xs[:, b, :]), over_groups(x_m),
                                        ALU.subtract).then_inc(shifted2, 1)

            def add_exps(b):
                dve.wait_ge(exp2_done, b + 1)
                dve.wait_ge(summed2, b - 1) if b > 1 else None
                nc.vector.tensor_tensor(x_sum, xs[:, b, :], xs[:, 0, :] if b == 1 else x_sum, ALU.add).then_inc(summed2, 1)

            shift(0)
            shift(1)
            for b in range(2, NB):
                shift(b)
                add_exps(b - 1)
            add_exps(NB - 1)
            dve.wait_ge(summed2, NB - 1)
            nc.vector.tensor_reduce(x_r, x_sum.rearrange("p (g q) -> p q g", q=P), AX.X, ALU.add).then_inc(sum2_folded, 1)
            dve.wait_ge(sum2_folded, 1)
            nc.vector.reciprocal(x_r, x_r).then_inc(sum2_folded, 1)
            dve.wait_ge(sum2_folded, 2)

            def weigh(b):
                nc.vector.tensor_tensor(by_group(xs[:, b, :]), by_group(xs[:, b, :]), over_groups(x_r),
                                        ALU.mult).then_inc(weights2_ready, 1)

            def add_attended(b):
                dve.wait_ge(pv2_done, b + 1)
                nc.vector.tensor_tensor(y[:, b, :].rearrange("p (d h) -> p d h", h=XH),
                                        banks[4 + b % 4].rearrange("p (h d) -> p d h", h=XH),
                                        y[:, b, :].rearrange("p (d h) -> p d h", h=XH), ALU.add).then_inc(attended2, 1)

            dve.wait_ge(normed, NB)
            weigh(0)
            for b in range(1, NB):
                weigh(b)
                add_attended(b - 1)
            add_attended(NB - 1)
            for first, count in LN_GROUPS[1]:
                layernorm_stats(1, first, count, attended2)
                layernorm_apply(1, first, count)

            steps = 0

            def then(ins):
                nonlocal steps
                steps += 1
                ins.then_inc(gate_step, 1)
                dve.wait_ge(gate_step, steps)

            def tiles_of(v, n):
                return v.unsqueeze(1).broadcast_to([P, NB, n])

            def across(v, n):
                return v.unsqueeze(2).broadcast_to([P, NB, n])

            dve.wait_ge(params_in, 64)
            dve.wait_ge(hidden_done, 1)
            then(nc.vector.tensor_tensor(hid, banks[0][:, 0:NB * GH].rearrange("p (b h) -> p b h", h=GH), tiles_of(gb1_b, GH), ALU.add))
            then(nc.vector.tensor_reduce(g_mean, hid, AX.X, ALU.add))
            then(nc.vector.tensor_scalar(g_mean, g_mean, 1.0 / GH, None, ALU.mult))
            then(nc.vector.tensor_tensor(hid, hid, across(g_mean, GH), ALU.subtract))
            then(nc.vector.tensor_tensor(hid_sq, hid, hid, ALU.mult))
            then(nc.vector.tensor_reduce(g_var, hid_sq, AX.X, ALU.add))
            nc.vector.tensor_scalar(g_var, g_var, 1.0 / GH, EPS, ALU.mult, ALU.add).then_inc(gate_var, 1)
            dve.wait_ge(gate_rstd, 1)
            then(nc.vector.tensor_tensor(hid, hid, across(g_rstd, GH), ALU.mult))
            then(nc.vector.tensor_tensor(hid, hid, tiles_of(gamma_b, GH), ALU.mult))
            then(nc.vector.tensor_tensor(hid, hid, tiles_of(beta_b, GH), ALU.add))
            nc.vector.tensor_scalar(hid, hid, 0.0, None, ALU.max).then_inc(hid_ready, 1)

            def add_main(b):
                dve.wait_ge(main_done, b + 1)
                nc.vector.tensor_tensor(y[:, b, :], banks[3 + b % 3], y[:, b, :], ALU.add).then_inc(main_added, 1)

            for b in range(4):
                add_main(b)
            dve.wait_ge(gates_done, 1)
            then(nc.vector.tensor_tensor(gates, banks[0][:, 0:NB * E].rearrange("p (b e) -> p b e", e=E), tiles_of(gb2_b, E), ALU.add))
            for b in range(NB):
                ins = nc.vector.max(top_v[:, b, :], gates[:, b, :])
            then(ins)
            for b in range(NB):
                ins = nc.vector.max_index(top_i[:, b, :], top_v[:, b, :], gates[:, b, :])
            then(ins)
            then(nc.vector.tensor_copy(top_f, top_i[:, :, 0:2]))
            for k in range(2):
                ins = nc.vector.tensor_tensor(onehot[:, :, k * E:(k + 1) * E], tiles_of(numbers, E),
                                              across(top_f[:, :, k], E), ALU.is_equal)
                ins.then_inc(onehot_ready, 1)
            nc.vector.tensor_tensor(g_diff, top_v[:, :, 1], top_v[:, :, 0], ALU.subtract).then_inc(diff_ready, 1)
            dve.wait_ge(e2_ready, 1)
            then(nc.vector.tensor_scalar(g_den, g_e2, 1.0, None, ALU.add))
            then(nc.vector.reciprocal(g_top[:, :, 0], g_den))
            then(nc.vector.tensor_tensor(g_top[:, :, 1], g_e2, g_top[:, :, 0], ALU.mult))
            dve.wait_ge(onehot_ready, 2)
            for k in range(2):
                ins = nc.vector.tensor_tensor(gated[:, :, k * E:(k + 1) * E], onehot[:, :, k * E:(k + 1) * E],
                                              across(g_top[:, :, k], E), ALU.mult)
            then(ins)
            dve.wait_ge(counted, 1)
            then(nc.vector.tensor_scalar(allowed, banks[0][:, 64:64 + 2 * E], CAPACITY, ALPHA, ALU.is_le, ALU.mult))
            then(nc.vector.tensor_tensor(gated, gated, tiles_of(allowed, 2 * E), ALU.mult))
            then(nc.vector.tensor_tensor(w_exp, gated[:, :, 0:E], gated[:, :, E:2 * E], ALU.add))
            dve.wait_ge(lora_a_done, 1)
            for k in range(2):
                nc.vector.tensor_tensor(tmp[:, 4 * k:4 * k + 4, :].rearrange("p b (e r) -> p (b e) r", r=R),
                                        banks[1 + k].rearrange("p (be r) -> p be r", r=R),
                                        w_exp[:, 4 * k:4 * k + 4, :].rearrange("p b e -> p (b e)").unsqueeze(2).broadcast_to([P, 4 * E, R]),
                                        ALU.mult).then_inc(tmp_ready, 1)
            for b in range(4, NB):
                add_main(b)
            for first, count in LN_GROUPS[2]:
                for b in range(first, first + count):
                    dve.wait_ge(lora_done, b + 1)
                    dve.wait_ge(main_added, b + 1)
                    nc.vector.tensor_tensor(y[:, b, :], banks[3 + b % 3], y[:, b, :], ALU.add).then_inc(lora_added, 1)
                layernorm_stats(2, first, count, lora_added)
                layernorm_apply(2, first, count)

        @block.tensor
        def _(pe):
            def project(j, p, half, c, groups=range(KC)):
                if half == 0 and 0 in groups:
                    wait(pe, w_ready, NT * j + c + 1)
                for g in groups:
                    u = KC * c + g
                    tile, grp = (c, g - 3) if g == 3 else (c - 1, g + 1)
                    if grp % 2 == 0:
                        wait(pe, act_scaled, 2 * (NT * p + tile) + grp // 2 + 1)
                    else:
                        wait(pe, dve_scaled, 2 * (NT * p + tile) + grp // 2 + 1)
                    for k, part in enumerate((x_hi, x_lo)):
                        mm = nc.tensor.matmul(proj_ps[u % 3][:, :], w_sb[:, c, g, :],
                                              part[:, g, half * HALF:(half + 1) * HALF],
                                              start=(k == 0), stop=(k == 1))
                    mm.then_inc(unit_done, 1)

            def scores(n, b, p):
                s = b % 2
                wait(pe, exp_done, n - 1)
                if b % BPH == 0:
                    wait(pe, rotated, RT * (p + 1))
                nc.tensor.matmul(score_ps[s][:, :], ident_b[:, :], mask_b[:, :, :].rearrange("p h k -> p (h k)"),
                                 start=True, stop=False)
                for h in range(QPK):
                    mm = nc.tensor.matmul(score_ps[s][:, h * P:(h + 1) * P], q_t[:, h, b * P:(b + 1) * P],
                                          k_t[:, b * P:(b + 1) * P], start=False, stop=(h == QPK - 1))
                mm.then_inc(scored, 1)

            def turn_probs(n, b, v_phase=None):
                s = b % 2
                wait(pe, probs_ready, n + 1)
                wait(pe, probs_t_ready, n)
                if v_phase is not None:
                    wait(pe, v_ready, v_phase + 1)
                for h in range(QPK):
                    mm = nc.tensor.transpose(turn_ps[:, h * P:(h + 1) * P], probs[:, s, h, :], ident)
                mm.then_inc(probs_turned, 1)

            def turn_v(n, p):
                wait(pe, tile_summed, NT * p + 2)
                wait(pe, probs_t_ready, n)
                for i in range(BPH):
                    mm = nc.tensor.transpose(turn_ps[:, i * P:(i + 1) * P], v_t[:, i * P:(i + 1) * P], ident)
                mm.then_inc(v_turned, 1)

            def weigh_v(n, b, p):
                s = b % 2
                wait(pe, probs_t_ready, n + 1)
                wait(pe, heads_ready, n)
                if b % BPH == 0:
                    wait(pe, v_ready, p + 1)
                nc.tensor.matmul(pv_ps[:, :], v_sb[:, b, :], probs_t[:, s, :, :].rearrange("p h q -> p (h q)"),
                                 start=True, stop=True).then_inc(pv_done, 1)

            def project_out(n, b, j, par, heads=range(QPK)):
                s = b % 2
                if 0 in heads:
                    wait(pe, heads_ready, n + 1)
                    wait(pe, y_added, n)
                    if b == 0:
                        wait(pe, wo_ready, QPK * (j + 1))
                for h in heads:
                    mm = nc.tensor.matmul(out_ps[:, :], heads_t[:, s, h, :], wo_of(par, h),
                                          start=(h == 0), stop=(h == QPK - 1))
                if QPK - 1 in heads:
                    mm.then_inc(out_done, 1)

            def phase(j, par, par_before, half, proj):
                f = 2 * j + half
                p = f + 1
                jp = j + half
                first, second = (0, 1), (2, 3)
                for s in range(BPH):
                    b = half * BPH + s
                    n = NB * j + b

                    def units(c, groups):
                        if proj:
                            project(jp, p, 1 - half, c, groups)

                    def out_heads(heads):
                        if b > 0:
                            project_out(n - 1, b - 1, j, par, heads)
                        elif not (isinstance(j, int) and j == 0):
                            project_out(n - 1, NB - 1, j - 1, par_before, heads)

                    if s < 3:
                        scores(n + 1, b + 1, f)
                        if proj and s == 2:
                            turn_v(n, p)
                        units(2 * s, first)
                        if s == 0:
                            out_heads((0, 1))
                        turn_probs(n, b, p if (proj and s == 2) else None)
                        units(2 * s, second)
                        if s < 2:
                            if s == 1:
                                out_heads((0, 1))
                            weigh_v(n, b, f)
                            units(2 * s + 1, first)
                            out_heads((2, 3))
                            units(2 * s + 1, second)
                        else:
                            out_heads((0,))
                            units(2 * s + 1, first)
                            out_heads((1,))
                            units(2 * s + 1, second)
                            out_heads((2,))
                            weigh_v(n, b, f)
                            out_heads((3,))
                    else:
                        turn_probs(n, b)
                        out_heads((0, 1))
                        weigh_v(n, b, f)
                        out_heads((2, 3))
                        if proj:
                            scores(n + 1, (b + 1) % NB, p)

            pe.wait_ge(x_hi_ready, KC)
            pe.wait_ge(x_lo_ready, KC)
            for c in range(NT):
                project(0, 0, 0, c)
            turn_v(0, 0)
            pe.wait_ge(mask_ready, 1 + QPK)
            scores(0, 0, 0)
            pe.wait_ge(x_hi_ready, 2 * KC)
            pe.wait_ge(x_lo_ready, 2 * KC)
            phase(0, 0, 1, 0, True)
            phase(0, 0, 1, 1, True)
            with pe.Fori(1, NKV - 1) as j:
                par = pe.snap(j % 2)
                par_before = pe.snap((j + 1) % 2)
                phase(j, par, par_before, 0, True)
                phase(j, par, par_before, 1, True)
            phase(NKV - 1, 1, 0, 0, True)
            phase(NKV - 1, 1, 0, 1, False)
            project_out(NKV * NB - 1, NB - 1, NKV - 1, 1)

            def channels_by_token(i, w, src, nt, half):
                wait(pe, proj2_copied, i - 2)
                for g in range(KC):
                    mm = nc.tensor.matmul(banks[i % 3], w[:, g, nt * P:(nt + 1) * P], src[:, g, half * HALF:(half + 1) * HALF],
                                          start=(g == 0), stop=(g == KC - 1))
                mm.then_inc(proj2_done, 1)

            def turn_x(layer, b):
                pe.wait_ge(normed, layer * NB + b + 1)
                wait(pe, x_t_ready, layer * NB + b - 1)
                for g in range(KC):
                    mm = nc.tensor.transpose(banks[5 + b % 2][:, g * P:(g + 1) * P], y[:, b, g * P:(g + 1) * P], ident)
                mm.then_inc(x_turned, 1)

            pe.wait_ge(k2_in, 16)
            pe.wait_ge(v2_in, 32 * KC)
            pe.wait_ge(dve_scaled, 2 * NT * 2 * NKV)
            for i in range(8):
                channels_by_token(i, wk2, ctx_t, i // 2, i % 2)
            for b in range(NB):
                turn_x(0, b)
            pe.wait_ge(q2_in, 16)
            pe.wait_ge(x_t_ready, NB)
            for i in range(8):
                channels_by_token(8 + i, wq2, x2_t, i // 2, i % 2)
            pe.wait_ge(proj2_copied, 16)
            for b in range(NB):
                wait(pe, scores2_copied, b - 1)
                for n in range(KC):
                    for i in range(4):
                        mm = nc.tensor.matmul(banks[4 * (b % 2) + i][:, n * P:(n + 1) * P],
                                              k2_t[32 * i:32 * i + 32, n, b * P:(b + 1) * P],
                                              q2_t[32 * i:32 * i + 32, n, b * P:(b + 1) * P], start=True, stop=True)
                mm.then_inc(scored2, 1)
            pe.wait_ge(ones_ready, 2)
            pe.wait_ge(params_in, 64)
            for b in range(NB):
                wait(pe, proj2_copied, 16 + b - 2)
                if b == 0:
                    pe.wait_ge(scores2_copied, NB)
                i = 16 + b
                nc.tensor.matmul(banks[i % 3], ones[0:1, :], bias_v[:, :], start=True, stop=False)
                for g in range(KC):
                    mm = nc.tensor.matmul(banks[i % 3], ctx_t[:, g, b * P:(b + 1) * P], wv2[:, g, :],
                                          start=False, stop=(g == KC - 1))
                mm.then_inc(proj2_done, 1)
            pe.wait_ge(proj2_copied, 24)
            for b in range(NB):
                pe.wait_ge(weights2_ready, b + 1)
                wait(pe, attended2, b - 3)
                for n in range(KC):
                    for i in range(4):
                        h = 4 * n + i
                        mm = nc.tensor.matmul(banks[4 + b % 4][:, h * XD:(h + 1) * XD],
                                              xs[:, b, (4 * i + n) * P:(4 * i + n + 1) * P],
                                              v2[:, b, h * XD:(h + 1) * XD], start=True, stop=True)
                mm.then_inc(pv2_done, 1)
            pe.wait_ge(attended2, NB)

            for b in range(NB):
                turn_x(1, b)
            pe.wait_ge(x_t_ready, 2 * NB)
            pe.wait_ge(experts_in, 64)

            def by_token(dst, w, b):
                for g in range(KC):
                    mm = nc.tensor.matmul(dst, x3_t[:, g, b * P:(b + 1) * P], w[:, g, :], start=(g == 0), stop=(g == KC - 1))
                return mm

            def main(b):
                wait(pe, main_added, b - 2)
                by_token(banks[3 + b % 3], w_main, b).then_inc(main_done, 1)

            for b in range(NB):
                mm = by_token(banks[0][:, b * GH:(b + 1) * GH], w_g1, b)
            mm.then_inc(hidden_done, 1)
            for b in range(NB):
                mm = by_token(banks[1 + b // 4][:, (b % 4) * ER:(b % 4 + 1) * ER], w_a, b)
            mm.then_inc(lora_a_done, 1)
            main(0)
            main(1)
            pe.wait_ge(hid_ready, 1)
            for b in range(NB):
                mm = nc.tensor.transpose(banks[6 + b // 4][0:GH, (b % 4) * P:(b % 4 + 1) * P], hid[:, b, :], ident)
            mm.then_inc(hid_turned, 1)
            main(2)
            pe.wait_ge(hid_t_ready, 2)
            for b in range(NB):
                mm = nc.tensor.matmul(banks[0][:, b * E:(b + 1) * E], hid_t[0:GH, b * P:(b + 1) * P], gw2_t[:, :],
                                      start=True, stop=True)
            mm.then_inc(gates_done, 1)
            main(3)
            main(4)
            pe.wait_ge(onehot_ready, 2)
            for b in range(NB):
                mm = nc.tensor.matmul(banks[0][:, 64:64 + 2 * E], ones[:, :], onehot[:, b, :], start=(b == 0), stop=(b == NB - 1))
            mm.then_inc(counted, 1)
            main(5)
            pe.wait_ge(tmp_ready, 2)
            for b in range(NB):
                mm = nc.tensor.transpose(banks[6 + b // 4][:, (b % 4) * P:(b % 4 + 1) * P], tmp[:, b, :], ident)
            mm.then_inc(tmp_turned, 1)
            main(6)
            main(7)
            pe.wait_ge(tmp_t_ready, 2)
            for b in range(NB):
                pe.wait_ge(main_added, NB)
                wait(pe, lora_added, b - 2)
                nc.tensor.matmul(banks[3 + b % 3], tmp_t[:, b * P:(b + 1) * P], w_b[:, :], start=True, stop=True).then_inc(lora_done, 1)


def constants():
    d = np.arange(P)
    inv = (np.float32(1.0) / np.float32(10000.0) ** (np.arange(0, P, 2, dtype=np.float32) / np.float32(P))).astype(np.float32)
    freqs = np.arange(P, dtype=np.float32)[:, None] * inv
    emb = np.concatenate([freqs, freqs], axis=-1).astype(np.float32)
    sign = np.where(d < P // 2, -1.0, 1.0).astype(np.float32)[:, None]
    mask = np.where(d[None, :] <= d[:, None], 0.0, NEG).astype(np.float32)
    return np.ascontiguousarray(np.stack([np.eye(P, dtype=np.float32), mask, np.cos(emb).T, np.sin(emb).T * sign], axis=1)).astype(np.float32)


def lay_out(i):
    i = {k: np.asarray(v) for k, v in i.items()}

    def by_chunk(w):
        return w.reshape(-1, P, w.shape[-1]).transpose(1, 0, 2)

    def qkv(q, k, v, rows):
        q = q.reshape(rows, NKV, QPK, P).transpose(1, 2, 0, 3)
        k = k.reshape(rows, NKV, 1, P).transpose(1, 2, 0, 3)
        v = v.reshape(rows, NKV, 1, P).transpose(1, 2, 0, 3)
        return np.concatenate([k, v, q], axis=1)

    a = {}
    tokens = i["x"].reshape(T, D)
    a["x_t"] = by_chunk(tokens.T)
    a["x"] = i["x"].transpose(1, 0, 2)
    w = qkv(i["L0_attn_qw_q"], i["L0_attn_qw_k"], i["L0_attn_qw_v"], D)
    a["qkv"] = w.reshape(NKV, NT, KC, P, P).transpose(0, 3, 1, 2, 4)
    s = qkv(i["L0_attn_scales_q"], i["L0_attn_scales_k"], i["L0_attn_scales_v"], KC)
    a["qkv_scales"] = s.transpose(3, 0, 1, 2).reshape(P, NKV * NT * KC)
    a["o"] = i["L0_attn_qw_o"].reshape(NKV, QPK, P, D).transpose(0, 2, 1, 3)
    a["o_scales"] = i["L0_attn_scales_o"].reshape(NKV, QPK, D)
    a["consts"] = constants()
    a["wq2"] = by_chunk(i["L0_xattn_Wq"].T)
    a["wk2"] = by_chunk(i["L0_xattn_Wk"].T)
    a["wv2"] = by_chunk(i["L0_xattn_Wv"].T)
    a["ctx_t"] = by_chunk(i["ctx_4096"].reshape(T, D).T)
    a["bias_qk"] = np.concatenate([i["L0_xattn_bq"].reshape(KC, P).T, i["L0_xattn_bk"].reshape(KC, P).T], axis=1)
    a["bias_v"] = i["L0_xattn_bv"].reshape(1, D)
    a["w_main"] = by_chunk(i["L0_ffn_weight"].T)
    a["w_a"] = by_chunk(i["L0_ffn_lora_A"].transpose(1, 0, 2).reshape(D, ER))
    a["w_g1"] = by_chunk(i["L0_ffn_gw1"].T)
    a["w_b"] = i["L0_ffn_lora_B"].reshape(ER, D)
    a["gw2_t"] = i["L0_ffn_gw2"].T
    a["params"] = np.concatenate([i["L0_ffn_gb1"], i["L0_ffn_ln_gamma"], i["L0_ffn_ln_beta"], i["L0_ffn_gb2"],
                                  np.arange(E, dtype=np.float32)])
    return {k: np.ascontiguousarray(v) for k, v in a.items()}


def kernel(**inputs):
    import concourse.bacc as _bacc
    from concourse.bass_utils import run_bass_kernel_spmd as _run

    nc = _bacc.Bacc("TRN2", target_bir_lowering=False, num_devices=1)
    arrays = {f"in_{k}": v for k, v in lay_out(inputs).items()}
    t = {k[3:]: nc.dram_tensor(k, v.shape, mybir.dt.from_np(v.dtype), kind="ExternalInput").ap() for k, v in arrays.items()}
    out = nc.dram_tensor("out", (P, NB, D), F32, kind="ExternalOutput").ap()
    build(nc, t, out)
    r = _run(nc, [arrays], core_ids=[0])
    return np.ascontiguousarray(r.results[0]["out"].transpose(1, 0, 2))
```

```python
from contextlib import ExitStack

import numpy as np

import concourse.bass as bass
from concourse import mybir

F32 = mybir.dt.float32
F32R = mybir.dt.float32r
BF16 = mybir.dt.bfloat16
I32 = mybir.dt.int32
U32 = mybir.dt.uint32
ALU = mybir.AluOpType
ACT = mybir.ActivationFunctionType
AX = mybir.AxisListType

P = 128
NB = 8
T = NB * P
D = 512
KC = D // P
NKV = 8
QPK = 4
NT = 2 + QPK
HALF = T // 2
BPH = NB // 2
ZERO = 8.0
SCALE = 1.0 / float(np.sqrt(P))
NEG = -3.0e38

XH = 16
XD = D // XH
XSCALE = 1.0 / float(np.sqrt(XD))
E = 8
R = 16
ER = E * R
GH = 4 * E
CAPACITY = float(int(3.0 * T / E))
ALPHA = 1.0 / R
EPS = 1e-5

LN_GROUPS = [[(0, 4), (4, 4)], [(0, 2), (2, 2), (4, 2), (6, 2)], [(0, 2), (2, 2), (4, 2), (6, 2)]]
PE_SUMS = 1
SLOT = [4, 5, 6, 7, 0, 1, 2, 3]
APART = 5
ROPE_TILES = [0, 2, 3, 4, 5]
ARENA = 34816


def wait(eng, sem, value):
    if isinstance(value, int) and value <= 0:
        return
    eng.wait_ge(sem, value)


def build(nc, t, out):
    with ExitStack() as ctx:
        def sb(name, shape, dt=F32):
            return ctx.enter_context(nc.sbuf_tensor(name, shape, dt))

        def sem(name):
            return ctx.enter_context(nc.semaphore(name))

        with ExitStack() as first:
            x_hi = first.enter_context(nc.sbuf_tensor("x_hi", [P, KC, T], F32R))
            x_lo = first.enter_context(nc.sbuf_tensor("x_lo", [P, KC, T], F32R))
        late = sb("late", [P, 2 * KC * T])
        w_sb = sb("w_sb", [P, NT, KC, P], F32R)
        y = sb("y", [P, NB, D])
        consts = sb("consts", [P, 4, P])
        ident = consts[:, 0, :]
        ident_b = sb("ident_b", [P, P], BF16)
        mask_b = sb("mask_b", [P, QPK, P], BF16)
        small = sb("small", [P, 512])
        arena = sb("arena", [P, ARENA])

        at = [0]

        def carve(*shape, base=None):
            n = int(np.prod(shape))
            if base is not None:
                at[0] = base
            a = at[0]
            at[0] += n
            assert at[0] <= ARENA, at[0]
            v = arena[:, a:a + n]
            if len(shape) == 2:
                return v.rearrange("p (a b) -> p a b", b=shape[1])
            if len(shape) == 3:
                return v.rearrange("p (a b c) -> p a b c", b=shape[1], c=shape[2])
            return v

        w_int = carve(NT * KC * P).bitcast(I32).rearrange("p (c g n) -> p c g n", c=NT, g=KC)
        wo = carve(2, QPK, D)
        wo_int = carve(QPK * D).bitcast(I32).rearrange("p (h n) -> p h n", h=QPK)
        wo_scale = carve(QPK, D)
        q_t = carve(QPK, T)
        k_t = carve(T)
        v_sb = carve(NB, P)
        sum_a = carve(2, HALF)
        sum_b = carve(2, HALF)
        raw = carve(2, HALF)
        turned = carve(2, HALF)
        raw_cos = carve(2, HALF)
        v_t = carve(HALF)
        probs = carve(2, QPK, P)
        probs_t = carve(2, QPK, P)
        heads_t = carve(2, QPK, P)
        scales = carve(NKV * NT * KC)

        def scale_of(j, c, g):
            return scales[:, bass.ds((NT * KC) * j + (KC * c + g), 1)]

        def wo_of(par, h):
            return wo[:, bass.ds(par, 1), h, :].rearrange("p a n -> p (a n)")

        cos = consts[:, 2, :]
        sin = consts[:, 3, :]

        def by_tile(v):
            return v.rearrange("p (b q) -> p b q", q=P)

        def every_tile(v):
            return v.unsqueeze(1).broadcast_to([P, BPH, P])

        x_stage = q_t

        row_max = small[:, 0:8].rearrange("p (s h) -> p s h", s=2)
        neg_max = small[:, 8:16].rearrange("p (s h) -> p s h", s=2)
        row_sum = small[:, 16:24].rearrange("p (s h) -> p s h", s=2)
        row_inv = small[:, 24:32].rearrange("p (s h) -> p s h", s=2)

        xs = carve(NB, XH * P, base=0)
        wk2 = carve(KC, D, base=0)
        wq2 = carve(KC, D)
        x2_t = carve(KC, T)
        q2_heads = carve(KC, 4, HALF, base=16384)
        v2 = carve(NB, D, base=20480)
        k2_t = carve(KC, T, base=24576)
        ctx_t = carve(KC, T)
        wv2 = carve(KC, D)
        x_max = late[:, 0:XH * P]
        x_sum = arena[:, 16384:16384 + 2048]
        att_t = late[:, XH * P:XH * P + 2 * D].rearrange("p (s n) -> p s n", s=2)
        x_m = small[:, 128:256]
        x_r = small[:, 256:384]
        x_part = small[:, 384:512]

        x3_t = carve(KC, T, base=16384)
        gate_tmp = carve(P * NB, base=24576)
        tmp = gate_tmp.rearrange("p (b er) -> p b er", b=NB)
        hid_sq = gate_tmp[:, 0:NB * GH].rearrange("p (b h) -> p b h", b=NB)
        tmp_t = carve(T)
        hid_t = carve(T)
        hid = carve(NB, GH)
        gates = carve(NB, E)
        top_v = carve(NB, E)
        top_i = carve(NB * E).bitcast(U32).rearrange("p (b e) -> p b e", e=E)
        top_f = carve(NB, 2)
        onehot = carve(NB, 2 * E)
        gated = carve(NB, 2 * E)
        w_exp = carve(NB, E)
        allowed = carve(2 * E)
        g_mean = carve(NB)
        g_var = carve(NB)
        g_rstd = carve(NB)
        g_diff = carve(NB)
        g_e2 = carve(NB)
        g_den = carve(NB)
        g_top = carve(NB, 2)
        assert at[0] <= 28672, at[0]
        w_main = carve(KC, D, base=28672)
        w_ga = carve(KC, GH + ER)
        w_b = carve(D)

        params = sb("params", [P, 3 * GH + E + E])
        gb1_b = params[:, 0:GH]
        gamma_b = params[:, GH:2 * GH]
        beta_b = params[:, 2 * GH:3 * GH]
        gb2_b = params[:, 3 * GH:3 * GH + E]
        numbers = params[:, 3 * GH + E:3 * GH + 2 * E]
        gw2_t = sb("gw2_t", [GH, E])
        bias_qk = sb("bias_qk", [P, 2 * KC])
        bias_v = sb("bias_v", [1, D])
        ones = sb("ones", [P, P])
        minus_half = sb("minus_half", [P, NB])
        stats = sb("stats", [P, NB, 6])
        mean_var = sb("mean_var", [P, NB, 2])
        var_eps = sb("var_eps", [P, NB])
        rstd = sb("rstd", [P, NB])

        ps = ctx.enter_context(nc.psum_tensor("ps", [P, 8, 512], F32))
        banks = [ps[:, i, :] for i in range(8)]
        proj_ps = banks[0:3]
        score_ps = banks[3:5]
        turn_ps = banks[5]
        pv_ps = banks[6]
        out_ps = banks[7]

        consts_in = sem("consts_in")
        x_in = [sem("x_first_half_in"), sem("x_second_half_in")]
        w_first_in = [sem(f"w_first_{c}_in") for c in range(NT)]
        y_in = sem("y_in")
        scales_in = sem("scales_in")
        w_in = sem("w_in")
        wo_first_in = sem("wo_first_in")
        wo_in = sem("wo_in")
        mask_ready = sem("mask_ready")
        x_hi_ready = sem("x_hi_ready")
        x_lo_ready = sem("x_lo_ready")
        w_ready = sem("w_ready")
        wo_ready = sem("wo_ready")
        unit_done = sem("unit_done")
        act_scaled = sem("act_scaled")
        dve_scaled = sem("dve_scaled")
        tile_summed = sem("tile_summed")
        turned_in = [sem("turned_even_in"), sem("turned_odd_in")]
        cos_done = sem("cos_done")
        sin_done = sem("sin_done")
        rotated = sem("rotated")
        v_turned = sem("v_turned")
        v_ready = sem("v_ready")
        scored = sem("scored")
        max_done = sem("max_done")
        neg_ready = sem("neg_ready")
        exp_done = sem("exp_done")
        inv_ready = sem("inv_ready")
        probs_ready = sem("probs_ready")
        probs_turned = sem("probs_turned")
        probs_t_ready = sem("probs_t_ready")
        pv_done = sem("pv_done")
        heads_ready = sem("heads_ready")
        out_done = sem("out_done")
        y_added = sem("y_added")
        stored = sem("stored")
        k2_in = sem("k2_in")
        q2_in = sem("q2_in")
        v2_in = sem("v2_in")
        params_in = sem("params_in")
        experts_in = sem("experts_in")
        ones_ready = sem("ones_ready")
        stats_done = sem("stats_done")
        tile_stats = sem("tile_stats")
        eps_added = sem("eps_added")
        rstd_ready = sem("rstd_ready")
        normed = sem("normed")
        x_turned = sem("x_turned")
        x_t_ready = sem("x_t_ready")
        proj2_done = sem("proj2_done")
        proj2_copied = sem("proj2_copied")
        scored2 = sem("scored2")
        scores2_copied = sem("scores2_copied")
        scores2_maxed = sem("scores2_maxed")
        max2_ready = sem("max2_ready")
        shifted2 = sem("shifted2")
        exp2_done = sem("exp2_done")
        summed2 = sem("summed2")
        part_summed = sem("part_summed")
        sum2_folded = sem("sum2_folded")
        weights2_ready = sem("weights2_ready")
        pv2_done = sem("pv2_done")
        heads_cleared = sem("heads_cleared")
        att_copied = sem("att_copied")
        att_turned = sem("att_turned")
        attended2 = sem("attended2")
        hidden_done = sem("hidden_done")
        main_done = sem("main_done")
        main_added = sem("main_added")
        gate_step = sem("gate_step")
        gate_var = sem("gate_var")
        gate_rstd = sem("gate_rstd")
        hid_ready = sem("hid_ready")
        hid_turned = sem("hid_turned")
        hid_t_ready = sem("hid_t_ready")
        gates_done = sem("gates_done")
        onehot_ready = sem("onehot_ready")
        counted = sem("counted")
        diff_ready = sem("diff_ready")
        e2_ready = sem("e2_ready")
        tmp_ready = sem("tmp_ready")
        tmp_turned = sem("tmp_turned")
        tmp_t_ready = sem("tmp_t_ready")
        lora_done = sem("lora_done")
        lora_added = sem("lora_added")

        block = ctx.enter_context(nc.Block())

        def att_bank(b):
            return banks[6 if b % 2 == 0 else 4]

        def turn2_bank(layer, b):
            return banks[5 + b % 2] if layer == 0 else banks[5]

        UNITS = NT * KC
        RT = len(ROPE_TILES)

        def turned_count(p, c):
            return 32 * (3 * p + c // 2 + 1) if c % 2 == 0 else 32 * (2 * p + (c - 3) // 2 + 1)

        def slot_rotated(p, c):
            before = {0: (-1, 3), 2: (0, 0), 4: (0, 1), 3: (-1, 4), 5: (0, 2)}[c]
            return RT * (p + before[0]) + before[1] + 1

        @block.sync
        def _(sp):
            def load_x(half):
                for g in range(KC):
                    sp.dma_start(x_stage[:, g, half * HALF:(half + 1) * HALF],
                                 t["x_t"][:, g, half * HALF:(half + 1) * HALF]).then_inc(x_in[half], 16)

            load_x(0)
            sp.dma_start(w_int[:, 0], t["qkv"][0][:, 0]).then_inc(w_first_in[0], 16)
            sp.dma_start(scales[:, :], t["qkv_scales"]).then_inc(scales_in, 16)
            for c in range(1, NT):
                sp.dma_start(w_int[:, c], t["qkv"][0][:, c]).then_inc(w_first_in[c], 16)
                if c == 1:
                    sp.dma_start(consts[:, :, :], t["consts"]).then_inc(consts_in, 16)
            load_x(1)

            def load_wo(j):
                wait(sp, wo_ready, QPK * j)
                sp.dma_start(wo_int[:, :, :], t["o"][j]).then_inc(wo_in, 16)
                sp.dma_start(wo_scale[:, :, :], t["o_scales"][j].partition_broadcast(P)).then_inc(wo_in, 16)

            def load_w(j):
                wait(sp, w_ready, NT * j)
                sp.dma_start(w_int[:, :, :, :], t["qkv"][j]).then_inc(w_in, 16)

            def turn(p, c):
                wait(sp, tile_summed, NT * p + c + 1)
                s = c % 2
                for a, b in ((0, 64), (64, 0)):
                    sp.dma_start(turned[a:a + 64, s, :], raw[b:b + 64, s, :]).then_inc(turned_in[s], 16)

            def turns(p):
                for c in ROPE_TILES:
                    turn(p, c)

            for h, c in enumerate(ROPE_TILES):
                if h < QPK:
                    sp.dma_start(wo_int[:, h, :], t["o"][0][:, h, :]).then_inc(wo_first_in, 16)
                turn(0, c)
                if h < QPK:
                    sp.dma_start(wo_scale[:, h, :], t["o_scales"][0][h].partition_broadcast(P)).then_inc(wo_first_in, 16)
            sp.dma_start(y[:, :, :], t["x"]).then_inc(y_in, 16)
            sp.dma_start(bias_qk[:, :], t["bias_qk"]).then_inc(params_in, 16)
            sp.dma_start(bias_v[:, :], t["bias_v"]).then_inc(params_in, 16)
            sp.dma_start(gw2_t[:, :], t["gw2_t"]).then_inc(params_in, 16)
            sp.dma_start(params[:, :], t["params"].partition_broadcast(P)).then_inc(params_in, 16)

            def iteration(j, last_w):
                load_wo(j + 1)
                turns(2 * j + 1)
                if not last_w:
                    load_w(j + 2)
                turns(2 * j + 2)

            load_w(1)
            load_wo(1)
            for g, c in enumerate(ROPE_TILES):
                turn(1, c)
                if g < KC:
                    sp.dma_start(ctx_t[:, g, :], t["ctx_t"][:, g, :]).then_inc(v2_in, 16)
            load_w(2)
            for g, c in enumerate(ROPE_TILES):
                turn(2, c)
                if g < KC:
                    sp.dma_start(wv2[:, g, :], t["wv2"][:, g, :]).then_inc(v2_in, 16)
            with sp.Fori(1, NKV - 2) as j:
                iteration(j, False)
            iteration(NKV - 2, True)
            turns(2 * NKV - 1)
            sp.wait_ge(w_ready, NT * NKV)
            sp.dma_start(wk2[:, :, :], t["wk2"]).then_inc(k2_in, 16)
            sp.wait_ge(wo_ready, QPK * NKV)
            sp.dma_start(wq2[:, :, :], t["wq2"]).then_inc(q2_in, 16)
            sp.wait_ge(proj2_done, 24)
            sp.dma_start(w_main[:, :, :], t["w_main"]).then_inc(experts_in, 16)
            sp.dma_start(w_ga[:, :, :], t["w_ga"]).then_inc(experts_in, 16)
            sp.dma_start(w_b[:, :], t["w_b"]).then_inc(experts_in, 16)
            for b in range(NB):
                sp.wait_ge(normed, 2 * NB + b + 1)
                sp.dma_start(out[:, b, :], y[:, b, :]).then_inc(stored, 16)
            sp.wait_ge(stored, 16 * NB)

        @block.gpsimd
        def _(pool):
            def convert(c):
                nc.gpsimd.tensor_scalar(w_sb[:, c], w_int[:, c], -ZERO, 1.0, ALU.add, ALU.mult).then_inc(w_ready, 1)

            def finish(p, c):
                s = c % 2
                wait(pool, dve_scaled, 2 * (NT * p + c + 1))
                if c == 1:
                    wait(pool, v_turned, p)
                    dst = v_t
                else:
                    wait(pool, rotated, slot_rotated(p, c))
                    dst = raw[:, s, :]
                nc.gpsimd.tensor_tensor(dst, sum_a[:, s, :], sum_b[:, s, :], ALU.add).then_inc(tile_summed, 1)
                if c != 1:
                    wait(pool, tile_summed, NT * p + c + 1)
                    nc.gpsimd.tensor_tensor(by_tile(raw_cos[:, s, :]), by_tile(dst), every_tile(cos), ALU.mult).then_inc(cos_done, 1)

            for c in range(NT):
                wait(pool, w_first_in[c], 16)
                convert(c)
            pool.wait_ge(consts_in, 16)
            for c in range(NT):
                finish(0, c)

            def iteration(j, more):
                if more:
                    wait(pool, w_in, 16 * (j + 1))
                for c in range(NT):
                    finish(2 * j + 1, c)
                    if more:
                        convert(c)
                if more:
                    for c in range(NT):
                        finish(2 * j + 2, c)

            iteration(0, True)
            with pool.Fori(1, NKV - 1) as j:
                iteration(j, True)
            iteration(NKV - 1, False)

            nc.gpsimd.memset(minus_half[:, :], -0.5).then_inc(ones_ready, 1)
            nc.gpsimd.memset(ones[:, :], 1.0).then_inc(ones_ready, 1)
            pool.wait_ge(ones_ready, 2)
            groups = 0

            def inverse_deviation(layer, first, count):
                nonlocal groups
                groups += 1
                pool.wait_ge(tile_stats, layer * NB + first + count)
                nc.gpsimd.tensor_scalar(var_eps[:, first:first + count], mean_var[:, first:first + count, 1], EPS, 1.0,
                                        ALU.add, ALU.mult).then_inc(eps_added, 1)
                pool.wait_ge(eps_added, groups)
                nc.gpsimd.tensor_tensor(rstd[:, first:first + count], var_eps[:, first:first + count],
                                        minus_half[:, 0:count], ALU.pow).then_inc(rstd_ready, 1)

            for first, count in LN_GROUPS[0]:
                inverse_deviation(0, first, count)
            nc.gpsimd.memset(q2_heads[:, :, :, :], 0.0).then_inc(heads_cleared, 1)
            for first, count in LN_GROUPS[1]:
                inverse_deviation(1, first, count)
            pool.wait_ge(gate_var, 1)
            nc.gpsimd.tensor_tensor(g_rstd, g_var, minus_half[:, :], ALU.pow).then_inc(gate_rstd, 1)
            for first, count in LN_GROUPS[2]:
                inverse_deviation(2, first, count)

        @block.scalar
        def _(act):
            def cut_x(half):
                act.wait_ge(x_in[half], 16 * KC)
                for g in range(KC):
                    nc.scalar.activation(x_hi[:, g, half * HALF:(half + 1) * HALF],
                                         x_stage[:, g, half * HALF:(half + 1) * HALF], ACT.Copy).then_inc(x_hi_ready, 1)

            cut_x(0)
            act.wait_ge(scales_in, 16)

            def scale_group(j, p, c, g):
                unit = UNITS * p + KC * c + g
                wait(act, unit_done, unit + 1)
                wait(act, tile_summed, NT * p + c - 1)
                dst = (sum_a if g == 0 else sum_b)[:, c % 2, :]
                nc.scalar.activation(dst, proj_ps[(KC * c + g) % 3][:, :], ACT.Copy,
                                     scale=scale_of(j, c, g)).then_inc(act_scaled, 1)

            def exps(n, b):
                s = b % 2
                wait(act, neg_ready, n + 1)
                wait(act, probs_turned, n - 1)
                for h in range(QPK):
                    last = nc.scalar.activation(probs[:, s, h, :], score_ps[s][:, h * P:(h + 1) * P], ACT.Exp,
                                                bias=neg_max[:, s, h:h + 1], scale=SCALE,
                                                accum_out=row_sum[:, s, h:h + 1])
                last.then_inc(exp_done, 1)

            def copy_probs(n, b):
                s = b % 2
                wait(act, probs_turned, n + 1)
                wait(act, pv_done, n - 1)
                nc.scalar.activation(probs_t[:, s, :, :].rearrange("p h q -> p (h q)"), turn_ps[:, :],
                                     ACT.Copy).then_inc(probs_t_ready, 1)

            def copy_heads(n, b):
                s = b % 2
                wait(act, pv_done, n + 1)
                wait(act, out_done, n - 1)
                nc.scalar.activation(heads_t[:, s, :, :].rearrange("p h q -> p (h q)"), pv_ps[:, :],
                                     ACT.Copy).then_inc(heads_ready, 1)

            def copy_v(p, half):
                wait(act, v_turned, p + 1)
                nc.scalar.activation(v_sb[:, half * BPH:(half + 1) * BPH, :].rearrange("p b d -> p (b d)"),
                                     turn_ps[:, :], ACT.Copy).then_inc(v_ready, 1)

            def phase(j, half, project):
                p = 2 * j + half + 1
                jp = j + half
                for s in range(BPH):
                    b = half * BPH + s
                    n = NB * j + b
                    nxt = (b + 1) % NB
                    if s < 3:
                        if project:
                            if s == 2:
                                copy_v(p, 1 - half)
                            scale_group(jp, p, 2 * s, 0)
                        if s == 0:
                            copy_probs(n, b)
                            if project:
                                scale_group(jp, p, 0, 2)
                            exps(n + 1, nxt)
                        else:
                            exps(n + 1, nxt)
                            copy_probs(n, b)
                            if project:
                                scale_group(jp, p, 2 * s, 2)
                        if project and s == 2:
                            scale_group(jp, p, 5, 0)
                            scale_group(jp, p, 5, 2)
                        copy_heads(n, b)
                        if project and s < 2:
                            for g in (0, 2):
                                scale_group(jp, p, 2 * s + 1, g)
                    else:
                        copy_probs(n, b)
                        copy_heads(n, b)
                        if project:
                            exps(n + 1, nxt)

            for c in range(NT):
                for g in (0, 2):
                    scale_group(0, 0, c, g)
                if c == 2:
                    cut_x(1)
            copy_v(0, 0)
            exps(0, 0)
            phase(0, 0, True)
            phase(0, 1, True)
            with act.Fori(1, NKV - 1) as j:
                phase(j, 0, True)
                phase(j, 1, True)
            phase(NKV - 1, 0, True)
            phase(NKV - 1, 1, False)
            act.wait_ge(params_in, 64)

            def copy_proj2(i, dst, bias=None):
                act.wait_ge(proj2_done, i + 1)
                if bias is None:
                    ins = nc.scalar.activation(dst, banks[i % 3], ACT.Copy)
                else:
                    ins = nc.scalar.activation(dst, banks[i % 3], ACT.Identity, bias=bias)
                ins.then_inc(proj2_copied, 1)

            def copy_x_t(layer, b, dst):
                act.wait_ge(x_turned, layer * NB + b + 1)
                nc.scalar.activation(dst[:, :, b * P:(b + 1) * P],
                                     turn2_bank(layer, b).rearrange("p (c q) -> p c q", c=KC), ACT.Copy).then_inc(x_t_ready, 1)

            def copy_q2(n, half):
                act.wait_ge(proj2_done, 8 + 4 * half + n + 1)
                for i in range(4):
                    rows = slice(32 * i, 32 * i + 32)
                    ins = nc.scalar.activation(q2_heads[rows, n, i, :], banks[(8 + 4 * half + n) % 3][rows, :], ACT.Identity,
                                               bias=bias_qk[rows, n:n + 1])
                ins.then_inc(proj2_copied, 1)

            def copy_scores2(b):
                act.wait_ge(scored2, b + 1)
                nc.scalar.activation(xs[:, SLOT[b], :], ps[:, 4 * (b % 2):4 * (b % 2) + 4, :].rearrange("p a n -> p (a n)"),
                                     ACT.Copy).then_inc(scores2_copied, 1)

            def exps2(b):
                act.wait_ge(shifted2, b + 1)
                nc.scalar.activation(xs[:, SLOT[b], :], xs[:, SLOT[b], :], ACT.Exp, scale=XSCALE).then_inc(exp2_done, 1)

            act.wait_ge(y_added, NKV * NB)
            for i in range(8):
                copy_proj2(i, k2_t[:, i // 2, (i % 2) * HALF:(i % 2 + 1) * HALF], bias_qk[:, 4 + i // 2:5 + i // 2])
                if i >= 4:
                    copy_x_t(0, i - 4, x2_t)
            act.wait_ge(heads_cleared, 1)
            for i in range(4):
                copy_x_t(0, BPH + i, x2_t)
                copy_q2(i, 0)
            for b in range(BPH):
                copy_scores2(b)
            for i in range(4):
                copy_q2(i, 1)
            for b in range(BPH, NB):
                copy_scores2(b)
            def copy_v2(b):
                copy_proj2(16 + b, v2[:, b, :])

            copy_v2(0)
            exps2(0)
            copy_v2(1)
            exps2(1)
            exps2(2)
            copy_v2(2)
            exps2(3)
            exps2(4)
            copy_v2(3)
            exps2(5)
            exps2(6)
            copy_v2(4)
            exps2(7)
            for b in range(5, NB):
                copy_v2(b)

            def copy_att(b):
                act.wait_ge(pv2_done, b + 1)
                wait(act, att_turned, b - 1)
                nc.scalar.activation(att_t[:, b % 2, :], att_bank(b), ACT.Copy).then_inc(att_copied, 1)

            for b in range(5):
                copy_att(b)
            copy_x_t(1, 0, x3_t)
            copy_x_t(1, 1, x3_t)
            copy_att(5)
            copy_att(6)
            copy_x_t(1, 2, x3_t)
            copy_x_t(1, 3, x3_t)
            copy_att(7)
            for b in range(4, NB):
                copy_x_t(1, b, x3_t)
            for k in range(2):
                act.wait_ge(hid_turned, 1)
                nc.scalar.activation(hid_t[0:GH, k * 512:(k + 1) * 512], banks[6 + k][0:GH, :], ACT.Copy).then_inc(hid_t_ready, 1)
            act.wait_ge(diff_ready, 1)
            nc.scalar.activation(g_e2, g_diff, ACT.Exp).then_inc(e2_ready, 1)
            for k in range(2):
                act.wait_ge(tmp_turned, 1)
                nc.scalar.activation(tmp_t[:, k * 512:(k + 1) * 512], banks[6 + k], ACT.Copy).then_inc(tmp_t_ready, 1)

        @block.vector
        def _(dve):
            def cut_x(half):
                part = slice(half * HALF, (half + 1) * HALF)
                for g in range(KC):
                    dve.wait_ge(x_hi_ready, KC * half + g + 1)
                    nc.vector.tensor_tensor(x_lo[:, g, part], x_stage[:, g, part], x_hi[:, g, part].bitcast(F32),
                                            ALU.subtract).then_inc(x_lo_ready, 1)

            cut_x(0)
            dve.wait_ge(consts_in, 16)
            nc.vector.tensor_copy(ident_b[:, :], ident).then_inc(mask_ready, 1)
            for h in range(QPK):
                nc.vector.tensor_copy(mask_b[:, h, :], consts[:, 1, :]).then_inc(mask_ready, 1)
            dve.wait_ge(scales_in, 16)

            def add_group(j, p, c, g):
                unit = UNITS * p + KC * c + g
                wait(dve, unit_done, unit + 1)
                wait(dve, act_scaled, 2 * (NT * p + c) + (g + 1) // 2)
                acc = (sum_a if g == 1 else sum_b)[:, c % 2, :]
                nc.vector.scalar_tensor_tensor(acc, proj_ps[(KC * c + g) % 3][:, :],
                                               scale_of(j, c, g), acc,
                                               ALU.mult, ALU.add).then_inc(dve_scaled, 1)

            def rotate(p, c, half):
                s, r = c % 2, ROPE_TILES.index(c)
                wait(dve, turned_in[s], turned_count(p, c))
                nc.vector.tensor_tensor(by_tile(turned[:, s, :]), by_tile(turned[:, s, :]), every_tile(sin),
                                        ALU.mult).then_inc(sin_done, 1)
                wait(dve, sin_done, RT * p + r + 1)
                wait(dve, cos_done, RT * p + r + 1)
                dst = (k_t if c == 0 else q_t[:, c - 2, :])[:, half * HALF:(half + 1) * HALF]
                nc.vector.tensor_tensor(dst, raw_cos[:, s, :], turned[:, s, :], ALU.add).then_inc(rotated, 1)

            def maxima(n, b):
                s = b % 2
                wait(dve, scored, n + 1)
                wait(dve, neg_ready, n - 1)
                nc.vector.tensor_reduce(row_max[:, s, :], score_ps[s][:, :].rearrange("p (h k) -> p h k", k=P),
                                        AX.X, ALU.max).then_inc(max_done, 1)
                wait(dve, max_done, n + 1)
                wait(dve, exp_done, n - 1)
                nc.vector.tensor_scalar(neg_max[:, s, :], row_max[:, s, :], -SCALE, None,
                                        ALU.mult).then_inc(neg_ready, 1)

            def normalise(n, b):
                s = b % 2
                wait(dve, exp_done, n + 1)
                wait(dve, probs_ready, n - 1)
                nc.vector.reciprocal(row_inv[:, s, :], row_sum[:, s, :]).then_inc(inv_ready, 1)
                wait(dve, inv_ready, n + 1)
                nc.vector.tensor_tensor(probs[:, s, :, :], probs[:, s, :, :],
                                        row_inv[:, s, :].unsqueeze(2).broadcast_to([P, QPK, P]), ALU.mult).then_inc(probs_ready, 1)

            def add_out(n, b):
                wait(dve, out_done, n + 1)
                wait(dve, y_added, n - NB + 1)
                nc.vector.tensor_tensor(y[:, b, :], out_ps[:, :], y[:, b, :], ALU.add).then_inc(y_added, 1)

            def convert_wo(j, par, h):
                wait(dve, wo_in, 32 * j)
                wait(dve, out_done, NB * (j - 1))
                nc.vector.scalar_tensor_tensor(wo_of(par, h), wo_int[:, h, :], -ZERO, wo_scale[:, h, :],
                                               ALU.add, ALU.mult).then_inc(wo_ready, 1)

            def phase(j, par, half, project):
                p = 2 * j + half + 1
                jp = j + half
                for s in range(BPH):
                    b = half * BPH + s
                    n = NB * j + b
                    nxt = (b + 1) % NB
                    if s < 3:
                        maxima(n + 1, nxt)
                        if project:
                            add_group(jp, p, 2 * s, 1)
                            if s > 0:
                                rotate(p, 2 * s - 2, 1 - half)
                            add_group(jp, p, 2 * s, 3)
                        normalise(n + 1, nxt)
                        if project:
                            add_group(jp, p, 2 * s + 1, 1)
                            if s == 2:
                                rotate(p, 3, 1 - half)
                            add_group(jp, p, 2 * s + 1, 3)
                        if not (isinstance(j, int) and j == 0 and b == 0):
                            add_out(n - 1, (b - 1) % NB)
                    else:
                        if project:
                            rotate(p, 4, 1 - half)
                        if convert_next(j):
                            for h in (2 * half, 2 * half + 1):
                                convert_wo(j + 1, par, h)
                        if project:
                            rotate(p, 5, 1 - half)
                        add_out(n - 1, b - 1)
                        if project:
                            maxima(n + 1, nxt)
                            normalise(n + 1, nxt)

            def convert_next(j):
                return not (isinstance(j, int) and j == NKV - 1)

            for c in range(NT):
                if c > 1 and c - 2 in ROPE_TILES:
                    rotate(0, c - 2, 0)
                for g in (1, 3):
                    add_group(0, 0, c, g)
                if c == 2:
                    cut_x(1)
            rotate(0, 4, 0)
            rotate(0, 5, 0)
            dve.wait_ge(wo_first_in, 32 * QPK)
            for h in range(QPK):
                convert_wo(0, 0, h)
            maxima(0, 0)
            normalise(0, 0)
            dve.wait_ge(y_in, 16)
            phase(0, 1, 0, True)
            phase(0, 1, 1, True)
            with dve.Fori(1, NKV - 1) as j:
                par = dve.snap((j + 1) % 2)
                phase(j, par, 0, True)
                phase(j, par, 1, True)
            phase(NKV - 1, 0, 0, True)
            phase(NKV - 1, 0, 1, False)
            add_out(NKV * NB - 1, NB - 1)
            rstds = 0

            def layernorm_stats(layer, first, count, after=None, value=0):
                for b in range(first, first + count):
                    if after is not None:
                        dve.wait_ge(after, value + b + 1)
                    nc.vector.bn_stats(stats[:, b, :], y[:, b, :]).then_inc(stats_done, 1)
                dve.wait_ge(rstd_ready, rstds)
                for b in range(first, first + count):
                    dve.wait_ge(stats_done, layer * NB + b + 1)
                    nc.vector.bn_aggr(mean_var[:, b, :], stats[:, b, :]).then_inc(tile_stats, 1)

            def layernorm_apply(layer, first, count):
                nonlocal rstds
                rstds += 1
                dve.wait_ge(rstd_ready, rstds)
                dve.wait_ge(tile_stats, layer * NB + first + count)
                for b in range(first, first + count):
                    nc.vector.tensor_scalar(y[:, b, :], y[:, b, :], mean_var[:, b, 0:1], rstd[:, b:b + 1],
                                            ALU.subtract, ALU.mult).then_inc(normed, 1)

            for first, count in LN_GROUPS[0]:
                layernorm_stats(0, first, count, y_added, (NKV - 1) * NB)
                layernorm_apply(0, first, count)

            for b in range(1, NB):
                dve.wait_ge(scores2_copied, b + 1)
                wait(dve, scores2_maxed, b - 1)
                nc.vector.tensor_tensor(x_max, xs[:, SLOT[b], :], xs[:, SLOT[0], :] if b == 1 else x_max,
                                        ALU.max).then_inc(scores2_maxed, 1)
            dve.wait_ge(scores2_maxed, NB - 1)
            nc.vector.tensor_reduce(x_m, x_max.rearrange("p (g q) -> p q g", q=P), AX.X, ALU.max).then_inc(max2_ready, 1)
            dve.wait_ge(max2_ready, 1)

            def over_groups(v):
                return v.unsqueeze(1).broadcast_to([P, 16, P])

            def by_group(v):
                return v.rearrange("p (g q) -> p g q", q=P)

            def shift(b):
                nc.vector.tensor_tensor(by_group(xs[:, SLOT[b], :]), by_group(xs[:, SLOT[b], :]), over_groups(x_m),
                                        ALU.subtract).then_inc(shifted2, 1)

            def add_exps(b):
                k = b - PE_SUMS
                dve.wait_ge(exp2_done, b + 1)
                wait(dve, summed2, k - 1)
                nc.vector.tensor_tensor(x_sum, xs[:, SLOT[b], :], xs[:, SLOT[b - 1], :] if k == 1 else x_sum,
                                        ALU.add).then_inc(summed2, 1)

            for b in range(NB):
                shift(b)
                if b >= PE_SUMS + 2:
                    add_exps(b - 1)
            dve.wait_ge(part_summed, 1)
            nc.vector.tensor_reduce(x_part, banks[7].rearrange("p (g q) -> p q g", q=P), AX.X, ALU.add).then_inc(sum2_folded, 1)
            add_exps(NB - 1)
            dve.wait_ge(summed2, NB - 1 - PE_SUMS)
            nc.vector.tensor_reduce(x_r, x_sum.rearrange("p (g q) -> p q g", q=P), AX.X, ALU.add).then_inc(sum2_folded, 1)
            dve.wait_ge(sum2_folded, 2)
            nc.vector.tensor_tensor(x_r, x_r, x_part, ALU.add).then_inc(sum2_folded, 1)
            dve.wait_ge(sum2_folded, 3)
            nc.vector.reciprocal(x_r, x_r).then_inc(sum2_folded, 1)
            dve.wait_ge(sum2_folded, 4)

            def weigh(b):
                nc.vector.tensor_tensor(by_group(xs[:, SLOT[b], :]), by_group(xs[:, SLOT[b], :]), over_groups(x_r),
                                        ALU.mult).then_inc(weights2_ready, 1)

            def add_attended(b):
                dve.wait_ge(att_turned, b + 1)
                nc.vector.tensor_tensor(y[:, b, :].rearrange("p (d h) -> p d h", h=XH),
                                        banks[7].rearrange("p (h d) -> p d h", h=XH),
                                        y[:, b, :].rearrange("p (d h) -> p d h", h=XH), ALU.add).then_inc(attended2, 1)

            def add_main(b):
                dve.wait_ge(main_done, b + 1)
                nc.vector.tensor_tensor(y[:, b, :], banks[3 + b % 2], y[:, b, :], ALU.add).then_inc(main_added, 1)

            dve.wait_ge(normed, NB)
            weigh(0)
            weigh(1)
            for b in range(2, NB):
                weigh(b)
                add_attended(b - 2)
                if b % 2 == 1:
                    layernorm_stats(1, b - 3, 2, attended2)
                elif b > 2:
                    layernorm_apply(1, b - 4, 2)
            add_attended(6)
            layernorm_apply(1, 4, 2)
            add_attended(7)
            layernorm_stats(1, 6, 2, attended2)
            layernorm_apply(1, 6, 2)

            steps = 0

            def then(ins):
                nonlocal steps
                steps += 1
                ins.then_inc(gate_step, 1)
                dve.wait_ge(gate_step, steps)

            def tiles_of(v, n):
                return v.unsqueeze(1).broadcast_to([P, NB, n])

            def across(v, n):
                return v.unsqueeze(2).broadcast_to([P, NB, n])

            dve.wait_ge(params_in, 64)

            def first_products(k):
                count = min(3, NB - 3 * k)
                return ps[:, k, 0:count * (GH + ER)].rearrange("p (b c) -> p b c", b=count), slice(3 * k, 3 * k + count), count

            for k in range(3):
                products, tiles, count = first_products(k)
                dve.wait_ge(hidden_done, tiles.stop)
                ins = nc.vector.tensor_tensor(hid[:, tiles, :], products[:, :, 0:GH],
                                              gb1_b.unsqueeze(1).broadcast_to([P, count, GH]), ALU.add)
            then(ins)
            then(nc.vector.tensor_reduce(g_mean, hid, AX.X, ALU.add))
            then(nc.vector.tensor_scalar(g_mean, g_mean, 1.0 / GH, None, ALU.mult))
            then(nc.vector.tensor_tensor(hid, hid, across(g_mean, GH), ALU.subtract))
            then(nc.vector.tensor_tensor(hid_sq, hid, hid, ALU.mult))
            then(nc.vector.tensor_reduce(g_var, hid_sq, AX.X, ALU.add))
            nc.vector.tensor_scalar(g_var, g_var, 1.0 / GH, EPS, ALU.mult, ALU.add).then_inc(gate_var, 1)
            add_main(0)
            dve.wait_ge(gate_rstd, 1)
            then(nc.vector.tensor_tensor(hid, hid, across(g_rstd, GH), ALU.mult))
            then(nc.vector.tensor_tensor(hid, hid, tiles_of(gamma_b, GH), ALU.mult))
            then(nc.vector.tensor_tensor(hid, hid, tiles_of(beta_b, GH), ALU.add))
            nc.vector.tensor_scalar(hid, hid, 0.0, None, ALU.max).then_inc(hid_ready, 1)

            add_main(1)
            add_main(2)
            dve.wait_ge(gates_done, 1)
            then(nc.vector.tensor_tensor(gates, banks[5][:, 0:NB * E].rearrange("p (b e) -> p b e", e=E), tiles_of(gb2_b, E), ALU.add))
            for b in range(NB):
                ins = nc.vector.max(top_v[:, b, :], gates[:, b, :])
            then(ins)
            for b in range(NB):
                ins = nc.vector.max_index(top_i[:, b, :], top_v[:, b, :], gates[:, b, :])
            then(ins)
            then(nc.vector.tensor_copy(top_f, top_i[:, :, 0:2]))
            for k in range(2):
                ins = nc.vector.tensor_tensor(onehot[:, :, k * E:(k + 1) * E], tiles_of(numbers, E),
                                              across(top_f[:, :, k], E), ALU.is_equal)
                ins.then_inc(onehot_ready, 1)
            nc.vector.tensor_tensor(g_diff, top_v[:, :, 1], top_v[:, :, 0], ALU.subtract).then_inc(diff_ready, 1)
            add_main(3)
            dve.wait_ge(e2_ready, 1)
            then(nc.vector.tensor_scalar(g_den, g_e2, 1.0, None, ALU.add))
            then(nc.vector.reciprocal(g_top[:, :, 0], g_den))
            then(nc.vector.tensor_tensor(g_top[:, :, 1], g_e2, g_top[:, :, 0], ALU.mult))
            dve.wait_ge(onehot_ready, 2)
            for k in range(2):
                ins = nc.vector.tensor_tensor(gated[:, :, k * E:(k + 1) * E], onehot[:, :, k * E:(k + 1) * E],
                                              across(g_top[:, :, k], E), ALU.mult)
            then(ins)
            dve.wait_ge(counted, 1)
            then(nc.vector.tensor_scalar(allowed, banks[5][:, 64:64 + 2 * E], CAPACITY, ALPHA, ALU.is_le, ALU.mult))
            then(nc.vector.tensor_tensor(gated, gated, tiles_of(allowed, 2 * E), ALU.mult))
            then(nc.vector.tensor_tensor(w_exp, gated[:, :, 0:E], gated[:, :, E:2 * E], ALU.add))
            for k in range(3):
                products, tiles, count = first_products(k)
                nc.vector.tensor_tensor(tmp[:, tiles, :].rearrange("p b (e r) -> p b e r", r=R),
                                        products[:, :, GH:].rearrange("p b (e r) -> p b e r", r=R),
                                        w_exp[:, tiles, :].unsqueeze(3).broadcast_to([P, count, E, R]),
                                        ALU.mult).then_inc(tmp_ready, 1)
            add_main(4)
            for k, (first, count) in enumerate(LN_GROUPS[2]):
                for b in range(first, first + count):
                    if b < APART:
                        dve.wait_ge(lora_done, b + 1)
                        dve.wait_ge(main_added, b + 1)
                        nc.vector.tensor_tensor(y[:, b, :], banks[b % 3], y[:, b, :], ALU.add).then_inc(lora_added, 1)
                    elif b > APART:
                        add_main(b)
                if k == 0:
                    add_main(APART)
                dve.wait_ge(lora_added, min(first + count, APART))
                if first + count > APART:
                    dve.wait_ge(main_added, first + count)
                layernorm_stats(2, first, count)
                if k > 0:
                    layernorm_apply(2, *LN_GROUPS[2][k - 1])
            layernorm_apply(2, *LN_GROUPS[2][-1])

        @block.tensor
        def _(pe):
            def project(j, p, half, c, groups=range(KC)):
                if half == 0 and 0 in groups:
                    wait(pe, w_ready, NT * j + c + 1)
                for g in groups:
                    u = KC * c + g
                    tile, grp = (c, g - 3) if g == 3 else (c - 1, g + 1)
                    if grp % 2 == 0:
                        wait(pe, act_scaled, 2 * (NT * p + tile) + grp // 2 + 1)
                    else:
                        wait(pe, dve_scaled, 2 * (NT * p + tile) + grp // 2 + 1)
                    for k, part in enumerate((x_hi, x_lo)):
                        mm = nc.tensor.matmul(proj_ps[u % 3][:, :], w_sb[:, c, g, :],
                                              part[:, g, half * HALF:(half + 1) * HALF],
                                              start=(k == 0), stop=(k == 1))
                    mm.then_inc(unit_done, 1)

            def scores(n, b, p):
                s = b % 2
                wait(pe, exp_done, n - 1)
                if b % BPH == 0:
                    wait(pe, rotated, RT * (p + 1))
                nc.tensor.matmul(score_ps[s][:, :], ident_b[:, :], mask_b[:, :, :].rearrange("p h k -> p (h k)"),
                                 start=True, stop=False)
                for h in range(QPK):
                    mm = nc.tensor.matmul(score_ps[s][:, h * P:(h + 1) * P], q_t[:, h, b * P:(b + 1) * P],
                                          k_t[:, b * P:(b + 1) * P], start=False, stop=(h == QPK - 1))
                mm.then_inc(scored, 1)

            def turn_probs(n, b, v_phase=None):
                s = b % 2
                wait(pe, probs_ready, n + 1)
                wait(pe, probs_t_ready, n)
                if v_phase is not None:
                    wait(pe, v_ready, v_phase + 1)
                for h in range(QPK):
                    mm = nc.tensor.transpose(turn_ps[:, h * P:(h + 1) * P], probs[:, s, h, :], ident)
                mm.then_inc(probs_turned, 1)

            def turn_v(n, p):
                wait(pe, tile_summed, NT * p + 2)
                wait(pe, probs_t_ready, n)
                for i in range(BPH):
                    mm = nc.tensor.transpose(turn_ps[:, i * P:(i + 1) * P], v_t[:, i * P:(i + 1) * P], ident)
                mm.then_inc(v_turned, 1)

            def weigh_v(n, b, p):
                s = b % 2
                wait(pe, probs_t_ready, n + 1)
                wait(pe, heads_ready, n)
                if b % BPH == 0:
                    wait(pe, v_ready, p + 1)
                nc.tensor.matmul(pv_ps[:, :], v_sb[:, b, :], probs_t[:, s, :, :].rearrange("p h q -> p (h q)"),
                                 start=True, stop=True).then_inc(pv_done, 1)

            def project_out(n, b, j, par, heads=range(QPK)):
                s = b % 2
                if 0 in heads:
                    wait(pe, heads_ready, n + 1)
                    wait(pe, y_added, n)
                    if b == 0:
                        wait(pe, wo_ready, QPK * (j + 1))
                for h in heads:
                    mm = nc.tensor.matmul(out_ps[:, :], heads_t[:, s, h, :], wo_of(par, h),
                                          start=(h == 0), stop=(h == QPK - 1))
                if QPK - 1 in heads:
                    mm.then_inc(out_done, 1)

            def phase(j, par, par_before, half, proj):
                f = 2 * j + half
                p = f + 1
                jp = j + half
                first, second = (0, 1), (2, 3)
                for s in range(BPH):
                    b = half * BPH + s
                    n = NB * j + b

                    def units(c, groups):
                        if proj:
                            project(jp, p, 1 - half, c, groups)

                    def out_heads(heads):
                        if b > 0:
                            project_out(n - 1, b - 1, j, par, heads)
                        elif not (isinstance(j, int) and j == 0):
                            project_out(n - 1, NB - 1, j - 1, par_before, heads)

                    if s < 3:
                        scores(n + 1, b + 1, f)
                        if proj and s == 2:
                            turn_v(n, p)
                        units(2 * s, first)
                        if s == 0:
                            out_heads((0, 1))
                        turn_probs(n, b, p if (proj and s == 2) else None)
                        units(2 * s, second)
                        if s < 2:
                            if s == 1:
                                out_heads((0, 1))
                            weigh_v(n, b, f)
                            units(2 * s + 1, first)
                            out_heads((2, 3))
                            units(2 * s + 1, second)
                        else:
                            out_heads((0,))
                            units(2 * s + 1, first)
                            out_heads((1,))
                            units(2 * s + 1, second)
                            out_heads((2,))
                            weigh_v(n, b, f)
                            out_heads((3,))
                    else:
                        turn_probs(n, b)
                        out_heads((0, 1))
                        weigh_v(n, b, f)
                        out_heads((2, 3))
                        if proj:
                            scores(n + 1, (b + 1) % NB, p)

            pe.wait_ge(x_hi_ready, KC)
            pe.wait_ge(x_lo_ready, KC)
            for c in range(NT):
                project(0, 0, 0, c)
            turn_v(0, 0)
            pe.wait_ge(mask_ready, 1 + QPK)
            scores(0, 0, 0)
            pe.wait_ge(x_hi_ready, 2 * KC)
            pe.wait_ge(x_lo_ready, 2 * KC)
            phase(0, 0, 1, 0, True)
            phase(0, 0, 1, 1, True)
            with pe.Fori(1, NKV - 1) as j:
                par = pe.snap(j % 2)
                par_before = pe.snap((j + 1) % 2)
                phase(j, par, par_before, 0, True)
                phase(j, par, par_before, 1, True)
            phase(NKV - 1, 1, 0, 0, True)
            phase(NKV - 1, 1, 0, 1, False)
            project_out(NKV * NB - 1, NB - 1, NKV - 1, 1)

            def channels_by_token(i, w, src, nt, half):
                wait(pe, proj2_copied, i - 2)
                for g in range(KC):
                    mm = nc.tensor.matmul(banks[i % 3], w[:, g, nt * P:(nt + 1) * P], src[:, g, half * HALF:(half + 1) * HALF],
                                          start=(g == 0), stop=(g == KC - 1))
                mm.then_inc(proj2_done, 1)

            def turn_x(layer, b):
                pe.wait_ge(normed, layer * NB + b + 1)
                wait(pe, x_t_ready, b - 1 if layer == 0 else NB + b)
                bank = turn2_bank(layer, b)
                for g in range(KC):
                    mm = nc.tensor.transpose(bank[:, g * P:(g + 1) * P], y[:, b, g * P:(g + 1) * P], ident)
                mm.then_inc(x_turned, 1)

            pe.wait_ge(k2_in, 16)
            pe.wait_ge(v2_in, 32 * KC)
            pe.wait_ge(dve_scaled, 2 * NT * 2 * NKV)
            for i in range(8):
                channels_by_token(i, wk2, ctx_t, i // 2, i % 2)
                if i >= 4:
                    turn_x(0, i - 4)

            pe.wait_ge(q2_in, 16)
            pe.wait_ge(x_t_ready, BPH)
            for i in range(4):
                turn_x(0, BPH + i)
                channels_by_token(8 + i, wq2, x2_t, i, 0)

            def scores2(b):
                wait(pe, scores2_copied, b - 1)
                q = slice((b % BPH) * P, (b % BPH + 1) * P)
                for n in range(KC):
                    mm = nc.tensor.matmul(banks[4 * (b % 2) + n].rearrange("p (i q) -> p i q", q=P),
                                          k2_t[:, n, b * P:(b + 1) * P], q2_heads[:, n, :, q], start=True, stop=True)
                mm.then_inc(scored2, 1)

            pe.wait_ge(proj2_copied, 12)
            pe.wait_ge(x_t_ready, NB)
            for b in range(BPH):
                scores2(b)
            pe.wait_ge(scores2_copied, BPH - 1)
            for i in range(4):
                channels_by_token(12 + i, wq2, x2_t, i, 1)
            pe.wait_ge(proj2_copied, 16)
            for b in range(BPH, NB):
                scores2(b)

            pe.wait_ge(ones_ready, 2)
            pe.wait_ge(params_in, 64)
            pe.wait_ge(scores2_copied, NB - 1)

            def values(b):
                i = 16 + b
                wait(pe, proj2_copied, i - 2)
                nc.tensor.matmul(banks[i % 3], ones[0:1, :], bias_v[:, :], start=True, stop=False)
                for g in range(KC):
                    mm = nc.tensor.matmul(banks[i % 3], ctx_t[:, g, b * P:(b + 1) * P], wv2[:, g, :],
                                          start=False, stop=(g == KC - 1))
                mm.then_inc(proj2_done, 1)

            def sum_exps(b):
                pe.wait_ge(exp2_done, b + 1)
                for i in range(4):
                    mm = nc.tensor.matmul(banks[7], ident, xs[:, SLOT[b], i * 512:(i + 1) * 512],
                                          start=(b == 0 and i == 0), stop=(b == PE_SUMS - 1 and i == 3))
                if b == PE_SUMS - 1:
                    mm.then_inc(part_summed, 1)

            for b in range(NB):
                values(b)
                if b >= NB - 1 - PE_SUMS and b < NB - 1:
                    sum_exps(b - (NB - 1 - PE_SUMS))

            pe.wait_ge(proj2_copied, 24)
            pe.wait_ge(sum2_folded, 1)

            def attend(b):
                pe.wait_ge(weights2_ready, b + 1)
                wait(pe, att_copied, b - 1)
                for n in range(KC):
                    for i in range(4):
                        h = 4 * n + i
                        mm = nc.tensor.matmul(att_bank(b)[32 * i:32 * i + 32, n * P:(n + 1) * P], v2[:, b, h * XD:(h + 1) * XD],
                                              xs[:, SLOT[b], h * P:(h + 1) * P], start=True, stop=True)
                mm.then_inc(pv2_done, 1)

            def turn_att(b):
                pe.wait_ge(att_copied, b + 1)
                wait(pe, attended2, b)
                for n in range(KC):
                    mm = nc.tensor.transpose(banks[7][:, n * P:(n + 1) * P], att_t[:, b % 2, n * P:(n + 1) * P], ident)
                mm.then_inc(att_turned, 1)

            def gate_and_lora(b):
                wait(pe, x_t_ready, NB + b + 1)
                for g in range(KC):
                    mm = nc.tensor.matmul(banks[b // 3][:, (b % 3) * (GH + ER):(b % 3 + 1) * (GH + ER)],
                                          x3_t[:, g, b * P:(b + 1) * P], w_ga[:, g, :], start=(g == 0), stop=(g == KC - 1))
                mm.then_inc(hidden_done, 1)

            def main(b, with_lora=False):
                wait(pe, x_t_ready, NB + b + 1)
                wait(pe, main_added, b - 1)
                for g in range(KC):
                    mm = nc.tensor.matmul(banks[3 + b % 2], x3_t[:, g, b * P:(b + 1) * P], w_main[:, g, :],
                                          start=(g == 0), stop=(g == KC - 1 and not with_lora))
                if not with_lora:
                    mm.then_inc(main_done, 1)

            def add_lora(b):
                pe.wait_ge(tmp_t_ready, b // 4 + 1)
                nc.tensor.matmul(banks[3 + b % 2], tmp_t[:, b * P:(b + 1) * P], w_b[:, :],
                                 start=False, stop=True).then_inc(main_done, 1)

            attend(0)
            attend(1)
            turn_att(0)
            attend(2)
            turn_att(1)
            attend(3)
            turn_att(2)
            attend(4)
            turn_x(1, 0)
            turn_att(3)
            turn_x(1, 1)
            pe.wait_ge(experts_in, 48)
            gate_and_lora(0)
            attend(5)
            turn_att(4)
            gate_and_lora(1)
            attend(6)
            turn_x(1, 2)
            turn_att(5)
            turn_x(1, 3)
            gate_and_lora(2)
            attend(7)
            turn_att(6)
            gate_and_lora(3)
            turn_att(7)
            turn_x(1, 4)
            turn_x(1, 5)
            gate_and_lora(4)
            gate_and_lora(5)
            turn_x(1, 6)
            turn_x(1, 7)
            gate_and_lora(6)
            gate_and_lora(7)
            main(0)
            main(1)
            pe.wait_ge(hid_ready, 1)
            pe.wait_ge(attended2, NB)
            for b in range(NB):
                mm = nc.tensor.transpose(banks[6 + b // 4][0:GH, (b % 4) * P:(b % 4 + 1) * P], hid[:, b, :], ident)
            mm.then_inc(hid_turned, 1)
            main(2)
            for b in range(NB):
                if b % 4 == 0:
                    pe.wait_ge(hid_t_ready, b // 4 + 1)
                mm = nc.tensor.matmul(banks[5][:, b * E:(b + 1) * E], hid_t[0:GH, b * P:(b + 1) * P], gw2_t[:, :],
                                      start=True, stop=True)
            mm.then_inc(gates_done, 1)
            main(3)
            pe.wait_ge(onehot_ready, 2)
            for b in range(NB):
                mm = nc.tensor.matmul(banks[5][:, 64:64 + 2 * E], ones[:, :], onehot[:, b, :], start=(b == 0), stop=(b == NB - 1))
            mm.then_inc(counted, 1)
            main(4)
            main(5, with_lora=True)
            pe.wait_ge(tmp_ready, 3)
            for b in range(NB):
                mm = nc.tensor.transpose(banks[6 + b // 4][:, (b % 4) * P:(b % 4 + 1) * P], tmp[:, b, :], ident)
            mm.then_inc(tmp_turned, 1)

            def lora(b):
                pe.wait_ge(tmp_t_ready, b // 4 + 1)
                wait(pe, lora_added, b - 2)
                nc.tensor.matmul(banks[b % 3], tmp_t[:, b * P:(b + 1) * P], w_b[:, :],
                                 start=True, stop=True).then_inc(lora_done, 1)

            lora(0)
            lora(1)
            add_lora(5)
            main(6, with_lora=True)
            add_lora(6)
            lora(2)
            lora(3)
            main(7, with_lora=True)
            lora(4)
            add_lora(7)


def constants():
    d = np.arange(P)
    inv = (np.float32(1.0) / np.float32(10000.0) ** (np.arange(0, P, 2, dtype=np.float32) / np.float32(P))).astype(np.float32)
    freqs = np.arange(P, dtype=np.float32)[:, None] * inv
    emb = np.concatenate([freqs, freqs], axis=-1).astype(np.float32)
    sign = np.where(d < P // 2, -1.0, 1.0).astype(np.float32)[:, None]
    mask = np.where(d[None, :] <= d[:, None], 0.0, NEG).astype(np.float32)
    return np.ascontiguousarray(np.stack([np.eye(P, dtype=np.float32), mask, np.cos(emb).T, np.sin(emb).T * sign], axis=1)).astype(np.float32)


def lay_out(i):
    i = {k: np.asarray(v) for k, v in i.items()}

    def by_chunk(w):
        return w.reshape(-1, P, w.shape[-1]).transpose(1, 0, 2)

    def qkv(q, k, v, rows):
        q = q.reshape(rows, NKV, QPK, P).transpose(1, 2, 0, 3)
        k = k.reshape(rows, NKV, 1, P).transpose(1, 2, 0, 3)
        v = v.reshape(rows, NKV, 1, P).transpose(1, 2, 0, 3)
        return np.concatenate([k, v, q], axis=1)

    a = {}
    tokens = i["x"].reshape(T, D)
    a["x_t"] = by_chunk(tokens.T)
    a["x"] = i["x"].transpose(1, 0, 2)
    w = qkv(i["L0_attn_qw_q"], i["L0_attn_qw_k"], i["L0_attn_qw_v"], D)
    a["qkv"] = w.reshape(NKV, NT, KC, P, P).transpose(0, 3, 1, 2, 4)
    s = qkv(i["L0_attn_scales_q"], i["L0_attn_scales_k"], i["L0_attn_scales_v"], KC)
    a["qkv_scales"] = s.transpose(3, 0, 1, 2).reshape(P, NKV * NT * KC)
    a["o"] = i["L0_attn_qw_o"].reshape(NKV, QPK, P, D).transpose(0, 2, 1, 3)
    a["o_scales"] = i["L0_attn_scales_o"].reshape(NKV, QPK, D)
    a["consts"] = constants()
    a["wq2"] = by_chunk(i["L0_xattn_Wq"].T)
    a["wk2"] = by_chunk(i["L0_xattn_Wk"].T)
    a["wv2"] = by_chunk(i["L0_xattn_Wv"].T)
    a["ctx_t"] = by_chunk(i["ctx_4096"].reshape(T, D).T)
    a["bias_qk"] = np.concatenate([i["L0_xattn_bq"].reshape(KC, P).T, i["L0_xattn_bk"].reshape(KC, P).T], axis=1)
    a["bias_v"] = i["L0_xattn_bv"].reshape(1, D)
    a["w_main"] = by_chunk(i["L0_ffn_weight"].T)
    a["w_ga"] = by_chunk(np.concatenate([i["L0_ffn_gw1"].T, i["L0_ffn_lora_A"].transpose(1, 0, 2).reshape(D, ER)], axis=1))
    a["w_b"] = i["L0_ffn_lora_B"].reshape(ER, D)
    a["gw2_t"] = i["L0_ffn_gw2"].T
    a["params"] = np.concatenate([i["L0_ffn_gb1"], i["L0_ffn_ln_gamma"], i["L0_ffn_ln_beta"], i["L0_ffn_gb2"],
                                  np.arange(E, dtype=np.float32)])
    return {k: np.ascontiguousarray(v) for k, v in a.items()}


def kernel(**inputs):
    import concourse.bacc as _bacc
    from concourse.bass_utils import run_bass_kernel_spmd as _run

    nc = _bacc.Bacc("TRN2", target_bir_lowering=False, num_devices=1)
    arrays = {f"in_{k}": v for k, v in lay_out(inputs).items()}
    t = {k[3:]: nc.dram_tensor(k, v.shape, mybir.dt.from_np(v.dtype), kind="ExternalInput").ap() for k, v in arrays.items()}
    out = nc.dram_tensor("out", (P, NB, D), F32, kind="ExternalOutput").ap()
    build(nc, t, out)
    r = _run(nc, [arrays], core_ids=[0])
    return np.ascontiguousarray(r.results[0]["out"].transpose(1, 0, 2))
```

```python
from contextlib import ExitStack

import numpy as np

import concourse.bass as bass
from concourse import mybir

F32 = mybir.dt.float32
F32R = mybir.dt.float32r
BF16 = mybir.dt.bfloat16
I32 = mybir.dt.int32
U32 = mybir.dt.uint32
ALU = mybir.AluOpType
ACT = mybir.ActivationFunctionType
AX = mybir.AxisListType

P = 128
NB = 8
T = NB * P
D = 512
KC = D // P
NKV = 8
QPK = 4
NT = 2 + QPK
HALF = T // 2
BPH = NB // 2
ZERO = 8.0
SCALE = 1.0 / float(np.sqrt(P))
NEG = -3.0e38

XH = 16
XD = D // XH
XSCALE = 1.0 / float(np.sqrt(XD))
E = 8
R = 16
ER = E * R
GH = 4 * E
CAPACITY = float(int(3.0 * T / E))
ALPHA = 1.0 / R
EPS = 1e-5

LN_GROUPS = [[(0, 4), (4, 4)], [(0, 2), (2, 2), (4, 2), (6, 2)], [(0, 2), (2, 2), (4, 2), (6, 2)]]
PE_SUMS = 2
SLOT = [4, 5, 6, 7, 0, 1, 2, 3]
APART = 5
ROPE_TILES = [0, 2, 3, 4, 5]
ARENA = 32768
HEADS_AT = 20480
OUTS = QPK * KC
ACT_TILES = 2
PRODUCTS = (
    "G0 G1 G2 G3 G4 G5 G6 O0 O1 G7 G8 G9 G10 G11 O2 O3 G12 G13 G14 G15 "
    "G16 G17 G18 G19 G20 O4 G21 G22 G23 O5 O6 O7 O8 O9 O10 O11 O12 O13 O14 O15").split()


def wait(eng, sem, value):
    if isinstance(value, int) and value <= 0:
        return
    eng.wait_ge(sem, value)


def build(nc, t, out):
    with ExitStack() as ctx:
        def sb(name, shape, dt=F32):
            return ctx.enter_context(nc.sbuf_tensor(name, shape, dt))

        def sem(name):
            return ctx.enter_context(nc.semaphore(name))

        with ExitStack() as first:
            x_hi = first.enter_context(nc.sbuf_tensor("x_hi", [P, KC, T], F32R))
            x_lo = first.enter_context(nc.sbuf_tensor("x_lo", [P, KC, T], F32R))
        late = sb("late", [P, 2 * KC * T])
        w_sb = sb("w_sb", [P, NT, KC, P], F32R)
        y = sb("y", [P, NB, D])
        consts = sb("consts", [P, 4, P])
        ident = consts[:, 0, :]
        ident_b = sb("ident_b", [P, P], BF16)
        mask_b = sb("mask_b", [P, QPK, P], BF16)
        small = sb("small", [P, 512])
        wo_sb = sb("wo_sb", [P, QPK, D], F32R)
        with ExitStack() as first:
            first.enter_context(nc.sbuf_tensor("before_heads", [P, HEADS_AT], F32))
            heads_hi = first.enter_context(nc.sbuf_tensor("heads_hi", [P, 2, QPK, HALF], F32R))
            heads_lo = first.enter_context(nc.sbuf_tensor("heads_lo", [P, 2, QPK, HALF], F32R))
        arena = sb("arena", [P, ARENA])

        at = [0]

        def carve(*shape, base=None):
            n = int(np.prod(shape))
            if base is not None:
                at[0] = base
            a = at[0]
            at[0] += n
            assert at[0] <= ARENA, at[0]
            v = arena[:, a:a + n]
            if len(shape) == 2:
                return v.rearrange("p (a b) -> p a b", b=shape[1])
            if len(shape) == 3:
                return v.rearrange("p (a b c) -> p a b c", b=shape[1], c=shape[2])
            return v

        w_int = carve(NT * KC * P).bitcast(I32).rearrange("p (c g n) -> p c g n", c=NT, g=KC)
        wo_int = carve(QPK * D).bitcast(I32).rearrange("p (h n) -> p h n", h=QPK)
        q_t = carve(QPK, T)
        k_t = carve(T)
        v_sb = carve(NB, P)
        sum_a = carve(2, HALF)
        sum_b = carve(2, HALF)
        raw = carve(2, HALF)
        turned = carve(2, HALF)
        raw_cos = carve(2, HALF)
        v_t = carve(HALF)
        probs = carve(2, QPK, P)
        probs_t = carve(2, QPK, P)
        out_part = carve(2, HALF)
        scales = carve(NKV * NT * KC)
        out_scales = carve(NKV * OUTS)
        assert at[0] <= HEADS_AT, at[0]

        def scale_of(j, c, g):
            return scales[:, bass.ds((NT * KC) * j + (KC * c + g), 1)]

        def out_scale_of(j, u):
            return out_scales[:, bass.ds(OUTS * j + u, 1)]

        def y_of(half, nt):
            return y[:, half * BPH:(half + 1) * BPH, nt * P:(nt + 1) * P]

        cos = consts[:, 2, :]
        sin = consts[:, 3, :]

        def by_tile(v):
            return v.rearrange("p (b q) -> p b q", q=P)

        def every_tile(v):
            return v.unsqueeze(1).broadcast_to([P, BPH, P])

        x_stage = q_t

        row_max = small[:, 0:8].rearrange("p (s h) -> p s h", s=2)
        neg_max = small[:, 8:16].rearrange("p (s h) -> p s h", s=2)
        row_sum = small[:, 16:24].rearrange("p (s h) -> p s h", s=2)
        row_inv = small[:, 24:32].rearrange("p (s h) -> p s h", s=2)

        xs = carve(NB, XH * P, base=0)
        wk2 = carve(KC, D, base=0)
        wq2 = carve(KC, D)
        x2_t = carve(KC, T)
        q2_heads = carve(KC, 4, HALF, base=16384)
        v2 = carve(NB, D, base=20480)
        wv2 = carve(KC, D, base=24576)
        ctx_t = carve(KC, T, base=28672)
        x_max = late[:, 0:XH * P]
        x_sum = arena[:, 16384:16384 + 2048]
        k2_t = late[:, 3072:3072 + KC * T].rearrange("p (a b) -> p a b", b=T)
        att_t = late[:, XH * P:XH * P + 2 * D].rearrange("p (s n) -> p s n", s=2)
        x_m = small[:, 128:256]
        x_r = small[:, 256:384]
        x_part = small[:, 384:512]

        x3_t = carve(KC, T, base=16384)
        late_at = [3072]

        def carve_late(*shape):
            n = int(np.prod(shape))
            v = late[:, late_at[0]:late_at[0] + n]
            late_at[0] += n
            return v.rearrange("p (a b) -> p a b", b=shape[1]) if len(shape) == 2 else v

        gate_tmp = carve_late(P * NB)
        tmp = gate_tmp.rearrange("p (b er) -> p b er", b=NB)
        hid_sq = gate_tmp[:, 0:NB * GH].rearrange("p (b h) -> p b h", b=NB)
        tmp_t = carve_late(T)
        hid_t = carve_late(T)
        hid = carve_late(NB, GH)
        gates = carve_late(NB, E)
        top_v = carve_late(NB, E)
        top_i = carve_late(NB * E).bitcast(U32).rearrange("p (b e) -> p b e", e=E)
        top_f = carve_late(NB, 2)
        onehot = carve_late(NB, 2 * E)
        gated = carve_late(NB, 2 * E)
        w_exp = carve_late(NB, E)
        allowed = carve_late(2 * E)
        g_mean = carve_late(NB)
        g_var = carve_late(NB)
        g_rstd = carve_late(NB)
        g_diff = carve_late(NB)
        g_e2 = carve_late(NB)
        g_den = carve_late(NB)
        g_top = carve_late(NB, 2)
        assert late_at[0] <= 2 * KC * T
        w_main = carve(KC, D, base=28672)
        w_ga = carve(KC, GH + ER)
        w_b = carve(D)

        params = sb("params", [P, 3 * GH + E + E])
        gb1_b = params[:, 0:GH]
        gamma_b = params[:, GH:2 * GH]
        beta_b = params[:, 2 * GH:3 * GH]
        gb2_b = params[:, 3 * GH:3 * GH + E]
        numbers = params[:, 3 * GH + E:3 * GH + 2 * E]
        gw2_t = sb("gw2_t", [GH, E])
        bias_qk = sb("bias_qk", [P, 2 * KC])
        bias_v = sb("bias_v", [1, D])
        ones = sb("ones", [P, P])
        minus_half = sb("minus_half", [P, NB])
        stats = sb("stats", [P, NB, 6])
        mean_var = sb("mean_var", [P, NB, 2])
        var_eps = sb("var_eps", [P, NB])
        rstd = sb("rstd", [P, NB])

        ps = ctx.enter_context(nc.psum_tensor("ps", [P, 8, 512], F32))
        banks = [ps[:, i, :] for i in range(8)]
        product_ps = [banks[0], banks[1], banks[2], banks[7]]
        score_ps = banks[3:5]
        turn_ps = banks[5]
        pv_ps = banks[6]

        consts_in = sem("consts_in")
        x_in = [sem("x_first_half_in"), sem("x_second_half_in")]
        w_first_in = [sem(f"w_first_{c}_in") for c in range(NT)]
        y_in = sem("y_in")
        scales_in = sem("scales_in")
        w_in = sem("w_in")
        out_scales_in = sem("out_scales_in")
        wo_in = sem("wo_in")
        mask_ready = sem("mask_ready")
        x_hi_ready = sem("x_hi_ready")
        x_lo_ready = sem("x_lo_ready")
        w_ready = sem("w_ready")
        wo_ready = sem("wo_ready")
        group_done = sem("group_done")
        act_scaled = sem("act_scaled")
        dve_scaled = sem("dve_scaled")
        tile_summed = sem("tile_summed")
        turned_in = [sem("turned_even_in"), sem("turned_odd_in")]
        cos_done = sem("cos_done")
        sin_done = sem("sin_done")
        rotated = sem("rotated")
        v_turned = sem("v_turned")
        v_ready = sem("v_ready")
        scored = sem("scored")
        max_done = sem("max_done")
        neg_ready = sem("neg_ready")
        exp_done = sem("exp_done")
        inv_ready = sem("inv_ready")
        probs_ready = sem("probs_ready")
        probs_turned = sem("probs_turned")
        probs_t_ready = sem("probs_t_ready")
        pv_done = sem("pv_done")
        heads_hi_ready = sem("heads_hi_ready")
        heads_ready = sem("heads_ready")
        out_done = sem("out_done")
        out_added = sem("out_added")
        out_scaled = sem("out_scaled")
        part_added = sem("part_added")
        y_turned = sem("y_turned")
        y_ready = sem("y_ready")
        stored = sem("stored")
        k2_in = sem("k2_in")
        q2_in = sem("q2_in")
        ctx_in = sem("ctx_in")
        v2_in = sem("v2_in")
        params_in = sem("params_in")
        experts_in = sem("experts_in")
        ones_ready = sem("ones_ready")
        stats_done = sem("stats_done")
        tile_stats = sem("tile_stats")
        eps_added = sem("eps_added")
        rstd_ready = sem("rstd_ready")
        normed = sem("normed")
        x_turned = sem("x_turned")
        x_t_ready = sem("x_t_ready")
        proj2_done = sem("proj2_done")
        proj2_copied = sem("proj2_copied")
        scored2 = sem("scored2")
        scores2_copied = sem("scores2_copied")
        scores2_maxed = sem("scores2_maxed")
        max2_ready = sem("max2_ready")
        shifted2 = sem("shifted2")
        exp2_done = sem("exp2_done")
        summed2 = sem("summed2")
        part_summed = sem("part_summed")
        sum2_folded = sem("sum2_folded")
        weights2_ready = sem("weights2_ready")
        pv2_done = sem("pv2_done")
        heads_cleared = sem("heads_cleared")
        att_copied = sem("att_copied")
        att_turned = sem("att_turned")
        attended2 = sem("attended2")
        hidden_done = sem("hidden_done")
        main_done = sem("main_done")
        main_added = sem("main_added")
        gate_step = sem("gate_step")
        gate_var = sem("gate_var")
        gate_rstd = sem("gate_rstd")
        hid_ready = sem("hid_ready")
        hid_turned = sem("hid_turned")
        hid_t_ready = sem("hid_t_ready")
        gates_done = sem("gates_done")
        onehot_ready = sem("onehot_ready")
        counted = sem("counted")
        diff_ready = sem("diff_ready")
        e2_ready = sem("e2_ready")
        tmp_ready = sem("tmp_ready")
        tmp_turned = sem("tmp_turned")
        tmp_t_ready = sem("tmp_t_ready")
        lora_done = sem("lora_done")
        lora_added = sem("lora_added")

        block = ctx.enter_context(nc.Block())

        DVE_TILES = KC - ACT_TILES

        def out_by_act(u):
            return u % KC >= DVE_TILES

        def act_index(u):
            return ACT_TILES * (u // KC) + u % KC - DVE_TILES

        def dve_index(u):
            return DVE_TILES * (u // KC) + u % KC

        def wait_out_read(eng, f, u):
            if out_by_act(u):
                wait(eng, out_scaled, ACT_TILES * QPK * (f - 1) + act_index(u) + 1)
            else:
                wait(eng, out_added, DVE_TILES * QPK * (f - 1) + dve_index(u) + 1)

        def product_bank(name):
            return product_ps[PRODUCTS.index(name) % 4]

        def out_bank(f, u):
            if isinstance(f, int) and f == 2 * NKV:
                return (product_ps[3], pv_ps)[u % 2]
            return product_bank(f"O{u}")

        def wait_product_bank(f, name):
            at, back = PRODUCTS.index(name) - 4, f
            while True:
                if at < 0:
                    at, back = at + len(PRODUCTS), back - 1
                before = PRODUCTS[at]
                if not isinstance(f, int) or (0 < back < 2 * NKV if before[0] == "O" else -1 <= back < 2 * NKV - 1):
                    break
                if back < -1:
                    return
                at -= 4
            u = int(before[1:])
            if before[0] == "O":
                wait_out_read(nc.tensor, back, u)
            else:
                sem = act_scaled if u % 2 == 0 else dve_scaled
                wait(nc.tensor, sem, 2 * (NT * (back + 1) + u // KC) + (u % KC) // 2 + 1)

        def att_bank(b):
            return banks[6 if b % 2 == 0 else 4]

        def turn2_bank(layer, b):
            return banks[5 + b % 2] if layer == 0 else banks[5]

        GROUPS = NT * KC
        RT = len(ROPE_TILES)

        def turned_count(p, c):
            return 32 * (3 * p + c // 2 + 1) if c % 2 == 0 else 32 * (2 * p + (c - 3) // 2 + 1)

        def slot_rotated(p, c):
            before = {0: (-1, 3), 2: (0, 0), 4: (0, 1), 3: (-1, 4), 5: (0, 2)}[c]
            return RT * (p + before[0]) + before[1] + 1

        @block.sync
        def _(sp):
            def load_x(half):
                for g in range(KC):
                    sp.dma_start(x_stage[:, g, half * HALF:(half + 1) * HALF],
                                 t["x_t"][:, g, half * HALF:(half + 1) * HALF]).then_inc(x_in[half], 16)

            load_x(0)
            sp.dma_start(w_int[:, 0], t["qkv"][0][:, 0]).then_inc(w_first_in[0], 16)
            sp.dma_start(scales[:, :], t["qkv_scales"]).then_inc(scales_in, 16)
            for c in range(1, NT):
                sp.dma_start(w_int[:, c], t["qkv"][0][:, c]).then_inc(w_first_in[c], 16)
                if c == 1:
                    sp.dma_start(consts[:, :, :], t["consts"]).then_inc(consts_in, 16)
            load_x(1)

            def load_wo_piece(j, k):
                if k == 0:
                    wait(sp, wo_ready, QPK * j)
                if k < QPK:
                    sp.dma_start(wo_int[:, k, :], t["o"][j][:, k, :]).then_inc(wo_in, 16)

            def load_w_pieces(j, tiles):
                if 0 in tiles:
                    wait(sp, w_ready, NT * j)
                for c in tiles:
                    sp.dma_start(w_int[:, c], t["qkv"][j][:, c]).then_inc(w_in, 16)

            def turn(p, c):
                wait(sp, tile_summed, NT * p + c + 1)
                s = c % 2
                for a, b in ((0, 64), (64, 0)):
                    sp.dma_start(turned[a:a + 64, s, :], raw[b:b + 64, s, :]).then_inc(turned_in[s], 16)

            def turns(p):
                for c in ROPE_TILES:
                    turn(p, c)

            turns(0)
            load_w_pieces(1, range(NT))
            sp.dma_start(out_scales[:, :], t["o_scales"]).then_inc(out_scales_in, 16)
            sp.dma_start(bias_qk[:, :], t["bias_qk"]).then_inc(params_in, 16)
            sp.dma_start(bias_v[:, :], t["bias_v"]).then_inc(params_in, 16)
            sp.dma_start(gw2_t[:, :], t["gw2_t"]).then_inc(params_in, 16)
            sp.dma_start(params[:, :], t["params"].partition_broadcast(P)).then_inc(params_in, 16)

            W_PIECES = [(0, 1), (2,), (3,), (4,), (5,)]

            def first_phase(j):
                for k, c in enumerate(ROPE_TILES):
                    turn(2 * j + 1, c)
                    load_wo_piece(j, k)
                    if isinstance(j, int) and j == 0 and k < BPH:
                        sp.dma_start(y[:, 2 * k:2 * k + 2, :], t["x"][:, 2 * k:2 * k + 2, :]).then_inc(y_in, 16)

            def second_phase(j, load):
                for k, c in enumerate(ROPE_TILES):
                    turn(2 * j + 2, c)
                    if load:
                        load_w_pieces(j + 2, W_PIECES[k])
                    if isinstance(j, int) and j == 0 and k < KC:
                        sp.dma_start(ctx_t[:, k, :], t["ctx_t"][:, k, :]).then_inc(ctx_in, 16)

            first_phase(0)
            second_phase(0, True)
            with sp.Fori(1, NKV - 2) as j:
                first_phase(j)
                second_phase(j, True)
            first_phase(NKV - 2)
            second_phase(NKV - 2, False)
            first_phase(NKV - 1)
            sp.wait_ge(w_ready, NT * NKV)
            sp.dma_start(wk2[:, :, :], t["wk2"]).then_inc(k2_in, 16)
            sp.wait_ge(wo_ready, QPK * NKV)
            sp.dma_start(wq2[:, :, :], t["wq2"]).then_inc(q2_in, 16)
            sp.wait_ge(out_done, OUTS * 2 * NKV)
            sp.dma_start(wv2[:, :, :], t["wv2"]).then_inc(v2_in, 16)
            sp.wait_ge(proj2_done, 24)
            sp.dma_start(w_main[:, :, :], t["w_main"]).then_inc(experts_in, 16)
            sp.dma_start(w_ga[:, :, :], t["w_ga"]).then_inc(experts_in, 16)
            sp.dma_start(w_b[:, :], t["w_b"]).then_inc(experts_in, 16)
            for b in range(NB):
                sp.wait_ge(normed, 2 * NB + b + 1)
                sp.dma_start(out[:, b, :], y[:, b, :]).then_inc(stored, 16)
            sp.wait_ge(stored, 16 * NB)

        @block.gpsimd
        def _(pool):
            def convert(c):
                nc.gpsimd.tensor_scalar(w_sb[:, c], w_int[:, c], -ZERO, 1.0, ALU.add, ALU.mult).then_inc(w_ready, 1)

            def finish(p, c):
                s = c % 2
                wait(pool, dve_scaled, 2 * (NT * p + c + 1))
                if c == 1:
                    wait(pool, v_turned, p)
                else:
                    wait(pool, rotated, slot_rotated(p, c))
                nc.gpsimd.tensor_tensor(v_t if c == 1 else raw[:, s, :], sum_a[:, s, :], sum_b[:, s, :],
                                        ALU.add).then_inc(tile_summed, 1)

            def times_cos(p, c):
                s = c % 2
                wait(pool, tile_summed, NT * p + c + 1)
                nc.gpsimd.tensor_tensor(by_tile(raw_cos[:, s, :]), by_tile(raw[:, s, :]), every_tile(cos), ALU.mult).then_inc(cos_done, 1)

            for c in range(NT):
                wait(pool, w_first_in[c], 16)
                convert(c)
            pool.wait_ge(consts_in, 16)
            for c in range(NT):
                finish(0, c)
                if c != 1:
                    times_cos(0, c)

            def add_part(f, u, half):
                k = act_index(u)
                wait(pool, out_scaled, ACT_TILES * QPK * (f - 1) + k + 1)
                wait(pool, part_added, ACT_TILES * QPK * (f - 1) + k + 1 - ACT_TILES)
                dst = y_of(half, u % KC)
                nc.gpsimd.tensor_tensor(dst, by_tile(out_part[:, k % 2, :]), dst, ALU.add).then_inc(part_added, 1)

            def phase(j, half, project, load):
                f = 2 * j + half

                def total(c):
                    if project:
                        finish(f + 1, c)

                def cosine(c):
                    if project:
                        times_cos(f + 1, c)

                def weights(c):
                    if load and half == 0:
                        convert(c)

                def outs(*products):
                    if not (isinstance(f, int) and f == 0):
                        for u in products:
                            add_part(f, u, 1 - half)

                if load and half == 0:
                    wait(pool, w_in, 16 * NT * (j + 1))
                total(0)
                cosine(0)
                weights(0)
                total(1)
                weights(1)
                outs(2)
                total(2)
                cosine(2)
                weights(2)
                total(3)
                outs(3)
                cosine(3)
                weights(3)
                total(4)
                cosine(4)
                weights(4)
                total(5)
                outs(6)
                cosine(5)
                outs(7, 10, 11, 14, 15)
                weights(5)

            phase(0, 0, True, True)
            pool.wait_ge(y_in, 16 * BPH)
            phase(0, 1, True, True)
            with pool.Fori(1, NKV - 1) as j:
                phase(j, 0, True, True)
                phase(j, 1, True, True)
            phase(NKV - 1, 0, True, False)
            phase(NKV - 1, 1, False, False)
            for u in range(OUTS):
                if out_by_act(u):
                    add_part(2 * NKV, u, 1)

            nc.gpsimd.memset(minus_half[:, :], -0.5).then_inc(ones_ready, 1)
            nc.gpsimd.memset(ones[:, :], 1.0).then_inc(ones_ready, 1)
            pool.wait_ge(ones_ready, 2)
            groups = 0

            def inverse_deviation(layer, first, count):
                nonlocal groups
                groups += 1
                pool.wait_ge(tile_stats, layer * NB + first + count)
                nc.gpsimd.tensor_scalar(var_eps[:, first:first + count], mean_var[:, first:first + count, 1], EPS, 1.0,
                                        ALU.add, ALU.mult).then_inc(eps_added, 1)
                pool.wait_ge(eps_added, groups)
                nc.gpsimd.tensor_tensor(rstd[:, first:first + count], var_eps[:, first:first + count],
                                        minus_half[:, 0:count], ALU.pow).then_inc(rstd_ready, 1)

            for first, count in LN_GROUPS[0]:
                inverse_deviation(0, first, count)
            nc.gpsimd.memset(q2_heads[:, :, :, :], 0.0).then_inc(heads_cleared, 1)
            for first, count in LN_GROUPS[1]:
                inverse_deviation(1, first, count)
            pool.wait_ge(gate_var, 1)
            nc.gpsimd.tensor_tensor(g_rstd, g_var, minus_half[:, :], ALU.pow).then_inc(gate_rstd, 1)
            for first, count in LN_GROUPS[2]:
                inverse_deviation(2, first, count)

        @block.scalar
        def _(act):
            def cut_x(half):
                act.wait_ge(x_in[half], 16 * KC)
                for g in range(KC):
                    nc.scalar.activation(x_hi[:, g, half * HALF:(half + 1) * HALF],
                                         x_stage[:, g, half * HALF:(half + 1) * HALF], ACT.Copy).then_inc(x_hi_ready, 1)

            cut_x(0)
            act.wait_ge(scales_in, 16)

            def scale_group(j, p, c, g):
                number = GROUPS * p + KC * c + g
                wait(act, group_done, number + 1)
                wait(act, tile_summed, NT * p + c - 1)
                dst = (sum_a if g == 0 else sum_b)[:, c % 2, :]
                nc.scalar.activation(dst, product_bank(f"G{KC * c + g}"), ACT.Copy,
                                     scale=scale_of(j, c, g)).then_inc(act_scaled, 1)

            def exps(n, b):
                s = b % 2
                wait(act, neg_ready, n + 1)
                wait(act, probs_turned, n - 1)
                for h in range(QPK):
                    last = nc.scalar.activation(probs[:, s, h, :], score_ps[s][:, h * P:(h + 1) * P], ACT.Exp,
                                                bias=neg_max[:, s, h:h + 1], scale=SCALE,
                                                accum_out=row_sum[:, s, h:h + 1])
                last.then_inc(exp_done, 1)

            def copy_probs(n, b):
                s = b % 2
                wait(act, probs_turned, n + 1)
                wait(act, pv_done, n - 1)
                nc.scalar.activation(probs_t[:, s, :, :].rearrange("p h q -> p (h q)"), turn_ps[:, :],
                                     ACT.Copy).then_inc(probs_t_ready, 1)

            def copy_heads(n, b, f):
                half, q = b // BPH, slice((b % BPH) * P, (b % BPH + 1) * P)
                wait(act, pv_done, n + 1)
                wait(act, out_done, OUTS * (f - 1))
                nc.scalar.activation(heads_hi[:, half, :, q], pv_ps.rearrange("p (h q) -> p h q", q=P),
                                     ACT.Copy).then_inc(heads_hi_ready, 1)

            def scale_out(j, f, u):
                k = act_index(u)
                wait(act, out_done, OUTS * (f - 1) + u + 1)
                wait(act, part_added, ACT_TILES * QPK * (f - 1) + k - 1)
                nc.scalar.activation(out_part[:, k % 2, :], out_bank(f, u), ACT.Copy,
                                     scale=out_scale_of(j, u)).then_inc(out_scaled, 1)

            def copy_v(p, half):
                wait(act, v_turned, p + 1)
                nc.scalar.activation(v_sb[:, half * BPH:(half + 1) * BPH, :].rearrange("p b d -> p (b d)"),
                                     turn_ps[:, :], ACT.Copy).then_inc(v_ready, 1)

            def phase(j, half, project):
                f = 2 * j + half
                n = NB * j + half * BPH

                def scale_groups(c, *groups):
                    if project:
                        for g in groups:
                            scale_group(j + half, f + 1, c, g)

                def exp(s):
                    if project or s < BPH:
                        exps(n + s, (half * BPH + s) % NB)

                def copy_turned(s):
                    copy_probs(n + s, half * BPH + s)

                def copy_head(s):
                    copy_heads(n + s, half * BPH + s, f)

                def copy_values():
                    if project:
                        copy_v(f + 1, 1 - half)

                def outs(*products):
                    if not (isinstance(f, int) and f == 0):
                        for u in products:
                            scale_out(j - 1 + half, f, u)

                scale_groups(0, 0, 2)
                scale_groups(1, 0, 2)
                copy_turned(0)
                exp(1)
                scale_groups(2, 0, 2)
                outs(2)
                copy_head(0)
                outs(3)
                scale_groups(3, 0, 2)
                exp(2)
                scale_groups(4, 0)
                copy_turned(1)
                scale_groups(4, 2)
                exp(3)
                scale_groups(5, 0, 2)
                copy_values()
                copy_head(1)
                copy_turned(2)
                outs(6)
                copy_head(2)
                outs(7)
                copy_turned(3)
                outs(10, 11, 14)
                copy_head(3)
                outs(15)
                exp(4)

            for c in range(NT):
                for g in (0, 2):
                    scale_group(0, 0, c, g)
            cut_x(1)
            copy_v(0, 0)
            exps(0, 0)
            act.wait_ge(out_scales_in, 16)
            phase(0, 0, True)
            phase(0, 1, True)
            with act.Fori(1, NKV - 1) as j:
                phase(j, 0, True)
                phase(j, 1, True)
            phase(NKV - 1, 0, True)
            phase(NKV - 1, 1, False)
            act.wait_ge(params_in, 64)

            def copy_proj2(i, dst, bias=None):
                act.wait_ge(proj2_done, i + 1)
                if bias is None:
                    ins = nc.scalar.activation(dst, banks[i % 3], ACT.Copy)
                else:
                    ins = nc.scalar.activation(dst, banks[i % 3], ACT.Identity, bias=bias)
                ins.then_inc(proj2_copied, 1)

            def copy_x_t(layer, b, dst):
                act.wait_ge(x_turned, layer * NB + b + 1)
                nc.scalar.activation(dst[:, :, b * P:(b + 1) * P],
                                     turn2_bank(layer, b).rearrange("p (c q) -> p c q", c=KC), ACT.Copy).then_inc(x_t_ready, 1)

            def copy_q2(n, half):
                act.wait_ge(proj2_done, 8 + 4 * half + n + 1)
                for i in range(4):
                    rows = slice(32 * i, 32 * i + 32)
                    ins = nc.scalar.activation(q2_heads[rows, n, i, :], banks[(8 + 4 * half + n) % 3][rows, :], ACT.Identity,
                                               bias=bias_qk[rows, n:n + 1])
                ins.then_inc(proj2_copied, 1)

            def copy_scores2(b):
                act.wait_ge(scored2, b + 1)
                nc.scalar.activation(xs[:, SLOT[b], :], ps[:, 4 * (b % 2):4 * (b % 2) + 4, :].rearrange("p a n -> p (a n)"),
                                     ACT.Copy).then_inc(scores2_copied, 1)

            def exps2(b):
                act.wait_ge(shifted2, b + 1)
                nc.scalar.activation(xs[:, SLOT[b], :], xs[:, SLOT[b], :], ACT.Exp, scale=XSCALE).then_inc(exp2_done, 1)

            def copy_y(b):
                act.wait_ge(y_turned, b + 1)
                nc.scalar.activation(y[:, b, :], score_ps[b % 2], ACT.Copy).then_inc(y_ready, 1)

            for i in range(8):
                copy_proj2(i, k2_t[:, i // 2, (i % 2) * HALF:(i % 2 + 1) * HALF], bias_qk[:, 4 + i // 2:5 + i // 2])
                if i < 4:
                    for u in range(4 * i, 4 * i + 4):
                        if out_by_act(u):
                            scale_out(NKV - 1, 2 * NKV, u)
                    copy_y(i)
                elif i < 6:
                    copy_y(2 * i - 4)
                    copy_y(2 * i - 3)
                else:
                    copy_x_t(0, 2 * i - 12, x2_t)
                    copy_x_t(0, 2 * i - 11, x2_t)
            act.wait_ge(heads_cleared, 1)
            for i in range(4):
                copy_x_t(0, BPH + i, x2_t)
                copy_q2(i, 0)
            for b in range(BPH):
                copy_scores2(b)
            for i in range(4):
                copy_q2(i, 1)
            for b in range(BPH, NB):
                copy_scores2(b)
            def copy_v2(b):
                copy_proj2(16 + b, v2[:, b, :])

            copy_v2(0)
            exps2(0)
            copy_v2(1)
            exps2(1)
            exps2(2)
            copy_v2(2)
            exps2(3)
            exps2(4)
            copy_v2(3)
            exps2(5)
            exps2(6)
            copy_v2(4)
            exps2(7)
            for b in range(5, NB):
                copy_v2(b)

            def copy_att(b):
                act.wait_ge(pv2_done, b + 1)
                wait(act, att_turned, b - 1)
                nc.scalar.activation(att_t[:, b % 2, :], att_bank(b), ACT.Copy).then_inc(att_copied, 1)

            for b in range(5):
                copy_att(b)
            copy_x_t(1, 0, x3_t)
            copy_x_t(1, 1, x3_t)
            copy_att(5)
            copy_att(6)
            copy_x_t(1, 2, x3_t)
            copy_x_t(1, 3, x3_t)
            copy_att(7)
            for b in range(4, NB):
                copy_x_t(1, b, x3_t)
            for k in range(2):
                act.wait_ge(hid_turned, 1)
                nc.scalar.activation(hid_t[0:GH, k * 512:(k + 1) * 512], banks[6 + k][0:GH, :], ACT.Copy).then_inc(hid_t_ready, 1)
            act.wait_ge(diff_ready, 1)
            nc.scalar.activation(g_e2, g_diff, ACT.Exp).then_inc(e2_ready, 1)
            for k in range(2):
                act.wait_ge(tmp_turned, 1)
                nc.scalar.activation(tmp_t[:, k * 512:(k + 1) * 512], banks[6 + k], ACT.Copy).then_inc(tmp_t_ready, 1)

        @block.vector
        def _(dve):
            def cut_x(half):
                part = slice(half * HALF, (half + 1) * HALF)
                for g in range(KC):
                    dve.wait_ge(x_hi_ready, KC * half + g + 1)
                    nc.vector.tensor_tensor(x_lo[:, g, part], x_stage[:, g, part], x_hi[:, g, part].bitcast(F32),
                                            ALU.subtract).then_inc(x_lo_ready, 1)

            cut_x(0)
            dve.wait_ge(consts_in, 16)
            nc.vector.tensor_copy(ident_b[:, :], ident).then_inc(mask_ready, 1)
            for h in range(QPK):
                nc.vector.tensor_copy(mask_b[:, h, :], consts[:, 1, :]).then_inc(mask_ready, 1)
            dve.wait_ge(scales_in, 16)

            def add_group(j, p, c, g):
                number = GROUPS * p + KC * c + g
                wait(dve, group_done, number + 1)
                wait(dve, act_scaled, 2 * (NT * p + c) + (g + 1) // 2)
                acc = (sum_a if g == 1 else sum_b)[:, c % 2, :]
                nc.vector.scalar_tensor_tensor(acc, product_bank(f"G{KC * c + g}"),
                                               scale_of(j, c, g), acc,
                                               ALU.mult, ALU.add).then_inc(dve_scaled, 1)

            def rotate(p, c, half):
                s, r = c % 2, ROPE_TILES.index(c)
                wait(dve, turned_in[s], turned_count(p, c))
                nc.vector.tensor_tensor(by_tile(turned[:, s, :]), by_tile(turned[:, s, :]), every_tile(sin),
                                        ALU.mult).then_inc(sin_done, 1)
                wait(dve, sin_done, RT * p + r + 1)
                wait(dve, cos_done, RT * p + r + 1)
                dst = (k_t if c == 0 else q_t[:, c - 2, :])[:, half * HALF:(half + 1) * HALF]
                nc.vector.tensor_tensor(dst, raw_cos[:, s, :], turned[:, s, :], ALU.add).then_inc(rotated, 1)

            def maxima(n, b):
                s = b % 2
                wait(dve, scored, n + 1)
                wait(dve, neg_ready, n - 1)
                nc.vector.tensor_reduce(row_max[:, s, :], score_ps[s][:, :].rearrange("p (h k) -> p h k", k=P),
                                        AX.X, ALU.max).then_inc(max_done, 1)
                wait(dve, max_done, n + 1)
                wait(dve, exp_done, n - 1)
                nc.vector.tensor_scalar(neg_max[:, s, :], row_max[:, s, :], -SCALE, None,
                                        ALU.mult).then_inc(neg_ready, 1)

            def normalise(n, b):
                s = b % 2
                wait(dve, exp_done, n + 1)
                wait(dve, probs_ready, n - 1)
                nc.vector.reciprocal(row_inv[:, s, :], row_sum[:, s, :]).then_inc(inv_ready, 1)
                wait(dve, inv_ready, n + 1)
                nc.vector.tensor_tensor(probs[:, s, :, :], probs[:, s, :, :],
                                        row_inv[:, s, :].unsqueeze(2).broadcast_to([P, QPK, P]), ALU.mult).then_inc(probs_ready, 1)

            def cut_heads(n, b):
                half, q = b // BPH, slice((b % BPH) * P, (b % BPH + 1) * P)
                wait(dve, heads_hi_ready, n + 1)
                nc.vector.tensor_tensor(heads_lo[:, half, :, q], pv_ps.rearrange("p (h q) -> p h q", q=P),
                                        heads_hi[:, half, :, q].bitcast(F32), ALU.subtract).then_inc(heads_ready, 1)

            def add_out(j, f, u, half):
                wait(dve, out_done, OUTS * (f - 1) + u + 1)
                wait(dve, out_added, DVE_TILES * QPK * (f - 1) + dve_index(u) + 1 - DVE_TILES)
                dst = y_of(half, u % KC)
                nc.vector.scalar_tensor_tensor(dst, by_tile(out_bank(f, u)),
                                               out_scale_of(j, u), dst, ALU.mult, ALU.add).then_inc(out_added, 1)

            def convert_wo(j, h):
                wait(dve, wo_in, 16 * QPK * (j + 1))
                wait(dve, out_done, OUTS * (2 * j - 1) + KC * (h + 1))
                nc.vector.tensor_scalar(wo_sb[:, h, :], wo_int[:, h, :], -ZERO, None, ALU.add).then_inc(wo_ready, 1)

            def phase(j, half, project):
                f = 2 * j + half
                n = NB * j + half * BPH

                def outs(*products):
                    if not (isinstance(f, int) and f == 0):
                        for u in products:
                            add_out(j - 1 + half, f, u, 1 - half)

                def add_groups(c, *groups):
                    if project:
                        for g in groups:
                            add_group(j + half, f + 1, c, g)

                def rotates(c):
                    if project:
                        rotate(f + 1, c, 1 - half)

                def maximum(s):
                    if project or s < BPH:
                        maxima(n + s, (half * BPH + s) % NB)

                def norm(s):
                    if project or s < BPH:
                        normalise(n + s, (half * BPH + s) % NB)

                def cut(s):
                    cut_heads(n + s, half * BPH + s)

                def weights(*heads):
                    if half == 0:
                        for h in heads:
                            convert_wo(j, h)

                add_groups(0, 1, 3)
                maximum(1)
                add_groups(1, 1)
                outs(0, 1)
                add_groups(1, 3)
                norm(1)
                add_groups(2, 1, 3)
                rotates(0)
                maximum(2)
                cut(0)
                add_groups(3, 1, 3)
                norm(2)
                maximum(3)
                add_groups(4, 1, 3)
                rotates(2)
                outs(4)
                add_groups(5, 1, 3)
                rotates(3)
                cut(1)
                outs(5, 8)
                norm(3)
                outs(9)
                cut(2)
                rotates(4)
                rotates(5)
                outs(12, 13)
                maximum(4)
                weights(0, 1)
                cut(3)
                weights(2, 3)
                norm(4)

            for c in range(NT):
                for g in (1, 3):
                    add_group(0, 0, c, g)
                if c > 1 and c - 2 in ROPE_TILES:
                    rotate(0, c - 2, 0)
            cut_x(1)
            rotate(0, 4, 0)
            rotate(0, 5, 0)
            maxima(0, 0)
            normalise(0, 0)
            phase(0, 0, True)
            dve.wait_ge(y_in, 16 * BPH)
            dve.wait_ge(out_scales_in, 16)
            phase(0, 1, True)
            with dve.Fori(1, NKV - 1) as j:
                phase(j, 0, True)
                phase(j, 1, True)
            phase(NKV - 1, 0, True)
            phase(NKV - 1, 1, False)
            for u in range(OUTS):
                if not out_by_act(u):
                    add_out(NKV - 1, 2 * NKV, u, 1)
            rstds = 0

            def layernorm_stats(layer, first, count, after=None, value=0):
                for b in range(first, first + count):
                    if after is not None:
                        dve.wait_ge(after, value + b + 1)
                    nc.vector.bn_stats(stats[:, b, :], y[:, b, :]).then_inc(stats_done, 1)
                dve.wait_ge(rstd_ready, rstds)
                for b in range(first, first + count):
                    dve.wait_ge(stats_done, layer * NB + b + 1)
                    nc.vector.bn_aggr(mean_var[:, b, :], stats[:, b, :]).then_inc(tile_stats, 1)

            def layernorm_apply(layer, first, count):
                nonlocal rstds
                rstds += 1
                dve.wait_ge(rstd_ready, rstds)
                dve.wait_ge(tile_stats, layer * NB + first + count)
                for b in range(first, first + count):
                    nc.vector.tensor_scalar(y[:, b, :], y[:, b, :], mean_var[:, b, 0:1], rstd[:, b:b + 1],
                                            ALU.subtract, ALU.mult).then_inc(normed, 1)

            for first, count in LN_GROUPS[0]:
                layernorm_stats(0, first, count, y_ready)
                layernorm_apply(0, first, count)

            for b in range(1, NB):
                dve.wait_ge(scores2_copied, b + 1)
                wait(dve, scores2_maxed, b - 1)
                nc.vector.tensor_tensor(x_max, xs[:, SLOT[b], :], xs[:, SLOT[0], :] if b == 1 else x_max,
                                        ALU.max).then_inc(scores2_maxed, 1)
            dve.wait_ge(scores2_maxed, NB - 1)
            nc.vector.tensor_reduce(x_m, x_max.rearrange("p (g q) -> p q g", q=P), AX.X, ALU.max).then_inc(max2_ready, 1)
            dve.wait_ge(max2_ready, 1)

            def over_groups(v):
                return v.unsqueeze(1).broadcast_to([P, 16, P])

            def by_group(v):
                return v.rearrange("p (g q) -> p g q", q=P)

            def shift(b):
                nc.vector.tensor_tensor(by_group(xs[:, SLOT[b], :]), by_group(xs[:, SLOT[b], :]), over_groups(x_m),
                                        ALU.subtract).then_inc(shifted2, 1)

            def add_exps(b):
                k = b - PE_SUMS
                dve.wait_ge(exp2_done, b + 1)
                wait(dve, summed2, k - 1)
                nc.vector.tensor_tensor(x_sum, xs[:, SLOT[b], :], xs[:, SLOT[b - 1], :] if k == 1 else x_sum,
                                        ALU.add).then_inc(summed2, 1)

            for b in range(NB):
                shift(b)
                if b >= PE_SUMS + 2:
                    add_exps(b - 1)
            dve.wait_ge(part_summed, 1)
            nc.vector.tensor_reduce(x_part, banks[7].rearrange("p (g q) -> p q g", q=P), AX.X, ALU.add).then_inc(sum2_folded, 1)
            add_exps(NB - 1)
            dve.wait_ge(summed2, NB - 1 - PE_SUMS)
            nc.vector.tensor_reduce(x_r, x_sum.rearrange("p (g q) -> p q g", q=P), AX.X, ALU.add).then_inc(sum2_folded, 1)
            dve.wait_ge(sum2_folded, 2)
            nc.vector.tensor_tensor(x_r, x_r, x_part, ALU.add).then_inc(sum2_folded, 1)
            dve.wait_ge(sum2_folded, 3)
            nc.vector.reciprocal(x_r, x_r).then_inc(sum2_folded, 1)
            dve.wait_ge(sum2_folded, 4)

            def weigh(b):
                nc.vector.tensor_tensor(by_group(xs[:, SLOT[b], :]), by_group(xs[:, SLOT[b], :]), over_groups(x_r),
                                        ALU.mult).then_inc(weights2_ready, 1)

            def add_attended(b):
                dve.wait_ge(att_turned, b + 1)
                nc.vector.tensor_tensor(y[:, b, :].rearrange("p (d h) -> p d h", h=XH),
                                        banks[7].rearrange("p (h d) -> p d h", h=XH),
                                        y[:, b, :].rearrange("p (d h) -> p d h", h=XH), ALU.add).then_inc(attended2, 1)

            def add_main(b):
                dve.wait_ge(main_done, b + 1)
                nc.vector.tensor_tensor(y[:, b, :], banks[3 + b % 2], y[:, b, :], ALU.add).then_inc(main_added, 1)

            dve.wait_ge(normed, NB)
            weigh(0)
            weigh(1)
            for b in range(2, NB):
                weigh(b)
                add_attended(b - 2)
                if b % 2 == 1:
                    layernorm_stats(1, b - 3, 2, attended2)
                elif b > 2:
                    layernorm_apply(1, b - 4, 2)
            add_attended(6)
            layernorm_apply(1, 4, 2)
            add_attended(7)
            layernorm_stats(1, 6, 2, attended2)
            layernorm_apply(1, 6, 2)

            steps = 0

            def then(ins):
                nonlocal steps
                steps += 1
                ins.then_inc(gate_step, 1)
                dve.wait_ge(gate_step, steps)

            def tiles_of(v, n):
                return v.unsqueeze(1).broadcast_to([P, NB, n])

            def across(v, n):
                return v.unsqueeze(2).broadcast_to([P, NB, n])

            dve.wait_ge(params_in, 64)

            def first_products(k):
                count = min(3, NB - 3 * k)
                return ps[:, k, 0:count * (GH + ER)].rearrange("p (b c) -> p b c", b=count), slice(3 * k, 3 * k + count), count

            for k in range(3):
                products, tiles, count = first_products(k)
                dve.wait_ge(hidden_done, tiles.stop)
                ins = nc.vector.tensor_tensor(hid[:, tiles, :], products[:, :, 0:GH],
                                              gb1_b.unsqueeze(1).broadcast_to([P, count, GH]), ALU.add)
            then(ins)
            then(nc.vector.tensor_reduce(g_mean, hid, AX.X, ALU.add))
            then(nc.vector.tensor_scalar(g_mean, g_mean, 1.0 / GH, None, ALU.mult))
            then(nc.vector.tensor_tensor(hid, hid, across(g_mean, GH), ALU.subtract))
            then(nc.vector.tensor_tensor(hid_sq, hid, hid, ALU.mult))
            then(nc.vector.tensor_reduce(g_var, hid_sq, AX.X, ALU.add))
            nc.vector.tensor_scalar(g_var, g_var, 1.0 / GH, EPS, ALU.mult, ALU.add).then_inc(gate_var, 1)
            add_main(0)
            dve.wait_ge(gate_rstd, 1)
            then(nc.vector.tensor_tensor(hid, hid, across(g_rstd, GH), ALU.mult))
            then(nc.vector.tensor_tensor(hid, hid, tiles_of(gamma_b, GH), ALU.mult))
            then(nc.vector.tensor_tensor(hid, hid, tiles_of(beta_b, GH), ALU.add))
            nc.vector.tensor_scalar(hid, hid, 0.0, None, ALU.max).then_inc(hid_ready, 1)

            add_main(1)
            add_main(2)
            dve.wait_ge(gates_done, 1)
            then(nc.vector.tensor_tensor(gates, banks[5][:, 0:NB * E].rearrange("p (b e) -> p b e", e=E), tiles_of(gb2_b, E), ALU.add))
            for b in range(NB):
                ins = nc.vector.max(top_v[:, b, :], gates[:, b, :])
            then(ins)
            for b in range(NB):
                ins = nc.vector.max_index(top_i[:, b, :], top_v[:, b, :], gates[:, b, :])
            then(ins)
            then(nc.vector.tensor_copy(top_f, top_i[:, :, 0:2]))
            for k in range(2):
                ins = nc.vector.tensor_tensor(onehot[:, :, k * E:(k + 1) * E], tiles_of(numbers, E),
                                              across(top_f[:, :, k], E), ALU.is_equal)
                ins.then_inc(onehot_ready, 1)
            nc.vector.tensor_tensor(g_diff, top_v[:, :, 1], top_v[:, :, 0], ALU.subtract).then_inc(diff_ready, 1)
            add_main(3)
            dve.wait_ge(e2_ready, 1)
            then(nc.vector.tensor_scalar(g_den, g_e2, 1.0, None, ALU.add))
            then(nc.vector.reciprocal(g_top[:, :, 0], g_den))
            then(nc.vector.tensor_tensor(g_top[:, :, 1], g_e2, g_top[:, :, 0], ALU.mult))
            dve.wait_ge(onehot_ready, 2)
            for k in range(2):
                ins = nc.vector.tensor_tensor(gated[:, :, k * E:(k + 1) * E], onehot[:, :, k * E:(k + 1) * E],
                                              across(g_top[:, :, k], E), ALU.mult)
            then(ins)
            dve.wait_ge(counted, 1)
            then(nc.vector.tensor_scalar(allowed, banks[5][:, 64:64 + 2 * E], CAPACITY, ALPHA, ALU.is_le, ALU.mult))
            then(nc.vector.tensor_tensor(gated, gated, tiles_of(allowed, 2 * E), ALU.mult))
            then(nc.vector.tensor_tensor(w_exp, gated[:, :, 0:E], gated[:, :, E:2 * E], ALU.add))
            for k in range(3):
                products, tiles, count = first_products(k)
                nc.vector.tensor_tensor(tmp[:, tiles, :].rearrange("p b (e r) -> p b e r", r=R),
                                        products[:, :, GH:].rearrange("p b (e r) -> p b e r", r=R),
                                        w_exp[:, tiles, :].unsqueeze(3).broadcast_to([P, count, E, R]),
                                        ALU.mult).then_inc(tmp_ready, 1)
            add_main(4)
            for k, (first, count) in enumerate(LN_GROUPS[2]):
                for b in range(first, first + count):
                    if b < APART:
                        dve.wait_ge(lora_done, b + 1)
                        dve.wait_ge(main_added, b + 1)
                        nc.vector.tensor_tensor(y[:, b, :], banks[b % 3], y[:, b, :], ALU.add).then_inc(lora_added, 1)
                    elif b > APART:
                        add_main(b)
                if k == 0:
                    add_main(APART)
                dve.wait_ge(lora_added, min(first + count, APART))
                if first + count > APART:
                    dve.wait_ge(main_added, first + count)
                layernorm_stats(2, first, count)
                if k > 0:
                    layernorm_apply(2, *LN_GROUPS[2][k - 1])
            layernorm_apply(2, *LN_GROUPS[2][-1])

        @block.tensor
        def _(pe):
            def project(j, p, half, c, groups=range(KC)):
                if half == 0 and 0 in groups:
                    wait(pe, w_ready, NT * j + c + 1)
                for g in groups:
                    u = KC * c + g
                    wait_product_bank(p - 1, f"G{u}")
                    for k, part in enumerate((x_hi, x_lo)):
                        mm = nc.tensor.matmul(product_bank(f"G{u}"), w_sb[:, c, g, :],
                                              part[:, g, half * HALF:(half + 1) * HALF],
                                              start=(k == 0), stop=(k == 1))
                    mm.then_inc(group_done, 1)

            def scores(n, b, p):
                s = b % 2
                wait(pe, exp_done, n - 1)
                if b % BPH == 0:
                    wait(pe, rotated, RT * (p + 1))
                nc.tensor.matmul(score_ps[s][:, :], ident_b[:, :], mask_b[:, :, :].rearrange("p h k -> p (h k)"),
                                 start=True, stop=False)
                for h in range(QPK):
                    mm = nc.tensor.matmul(score_ps[s][:, h * P:(h + 1) * P], q_t[:, h, b * P:(b + 1) * P],
                                          k_t[:, b * P:(b + 1) * P], start=False, stop=(h == QPK - 1))
                mm.then_inc(scored, 1)

            def turn_probs(n, b, v_phase=None):
                s = b % 2
                wait(pe, probs_ready, n + 1)
                wait(pe, probs_t_ready, n)
                if v_phase is not None:
                    wait(pe, v_ready, v_phase + 1)
                for h in range(QPK):
                    mm = nc.tensor.transpose(turn_ps[:, h * P:(h + 1) * P], probs[:, s, h, :], ident)
                mm.then_inc(probs_turned, 1)

            def turn_v(n, p):
                wait(pe, tile_summed, NT * p + 2)
                wait(pe, probs_t_ready, n)
                for i in range(BPH):
                    mm = nc.tensor.transpose(turn_ps[:, i * P:(i + 1) * P], v_t[:, i * P:(i + 1) * P], ident)
                mm.then_inc(v_turned, 1)

            def weigh_v(n, b, p):
                s = b % 2
                wait(pe, probs_t_ready, n + 1)
                wait(pe, heads_ready, n)
                if b % BPH == 0:
                    wait(pe, v_ready, p + 1)
                nc.tensor.matmul(pv_ps[:, :], v_sb[:, b, :], probs_t[:, s, :, :].rearrange("p h q -> p (h q)"),
                                 start=True, stop=True).then_inc(pv_done, 1)

            def project_out(f, u, half):
                h, nt = u // KC, u % KC
                if u == 0:
                    wait(pe, heads_ready, BPH * f)
                if not (isinstance(f, int) and f == 2 * NKV):
                    wait_product_bank(f, f"O{u}")
                elif u < 2:
                    wait_out_read(pe, f - 1, OUTS - 1)
                    wait_out_read(pe, f - 1, OUTS - 1 - ACT_TILES)
                else:
                    wait_out_read(pe, f, u - 2)
                for k, part in enumerate((heads_hi, heads_lo)):
                    mm = nc.tensor.matmul(out_bank(f, u), wo_sb[:, h, nt * P:(nt + 1) * P], part[:, half, h, :],
                                          start=(k == 0), stop=(k == 1))
                mm.then_inc(out_done, 1)

            def phase(j, half, proj):
                f = 2 * j + half
                n = NB * j + half * BPH

                def groups(c, *which):
                    if proj:
                        project(j + half, f + 1, 1 - half, c, which)

                def outs(*products):
                    if not (isinstance(f, int) and f == 0):
                        for u in products:
                            if u == 0:
                                wait(pe, wo_ready, QPK * (j + half))
                            project_out(f, u, 1 - half)

                def score(s):
                    if proj or s < BPH:
                        scores(n + s, (half * BPH + s) % NB, f + s // BPH)

                def turn_values():
                    if proj:
                        turn_v(n + 2, f + 1)

                def turn(s):
                    turn_probs(n + s, half * BPH + s, f + 1 if (proj and s == 2) else None)

                def weigh(s):
                    weigh_v(n + s, half * BPH + s, f)

                groups(0, 0, 1)
                score(1)
                groups(0, 2, 3)
                score(2)
                groups(1, 0, 1, 2)
                outs(0)
                turn(0)
                outs(1)
                groups(1, 3)
                groups(2, 0, 1, 2, 3)
                outs(2)
                weigh(0)
                outs(3)
                groups(3, 0, 1, 2, 3)
                score(3)
                groups(4, 0)
                turn(1)
                groups(4, 1, 2, 3)
                groups(5, 0)
                turn_values()
                weigh(1)
                outs(4)
                groups(5, 1, 2, 3)
                turn(2)
                outs(5, 6, 7, 8)
                weigh(2)
                outs(9)
                turn(3)
                outs(10, 11, 12, 13, 14)
                weigh(3)
                outs(15)
                score(4)

            pe.wait_ge(x_hi_ready, KC)
            pe.wait_ge(x_lo_ready, KC)
            for c in range(NT):
                project(0, 0, 0, c)
            turn_v(0, 0)
            pe.wait_ge(mask_ready, 1 + QPK)
            scores(0, 0, 0)
            pe.wait_ge(x_hi_ready, 2 * KC)
            pe.wait_ge(x_lo_ready, 2 * KC)
            phase(0, 0, True)
            phase(0, 1, True)
            with pe.Fori(1, NKV - 1) as j:
                phase(j, 0, True)
                phase(j, 1, True)
            phase(NKV - 1, 0, True)
            phase(NKV - 1, 1, False)

            def channels_by_token(i, w, src, nt, half):
                wait(pe, proj2_copied, i - 2)
                for g in range(KC):
                    mm = nc.tensor.matmul(banks[i % 3], w[:, g, nt * P:(nt + 1) * P], src[:, g, half * HALF:(half + 1) * HALF],
                                          start=(g == 0), stop=(g == KC - 1))
                mm.then_inc(proj2_done, 1)

            def turn_x(layer, b):
                pe.wait_ge(normed, layer * NB + b + 1)
                wait(pe, x_t_ready, b - 1 if layer == 0 else NB + b)
                bank = turn2_bank(layer, b)
                for g in range(KC):
                    mm = nc.tensor.transpose(bank[:, g * P:(g + 1) * P], y[:, b, g * P:(g + 1) * P], ident)
                mm.then_inc(x_turned, 1)

            pe.wait_ge(k2_in, 16)
            pe.wait_ge(ctx_in, 16 * KC)
            pe.wait_ge(dve_scaled, 2 * NT * 2 * NKV)
            wait_out_read(pe, 2 * NKV - 1, OUTS - 1)
            wait_out_read(pe, 2 * NKV - 1, OUTS - 1 - ACT_TILES)

            def turn_y(b):
                last = 2 * NKV - 1 + b // BPH
                pe.wait_ge(out_added, DVE_TILES * QPK * last)
                pe.wait_ge(part_added, ACT_TILES * QPK * last)
                wait(pe, y_ready, b - 1)
                for nt in range(KC):
                    mm = nc.tensor.transpose(score_ps[b % 2][:, nt * P:(nt + 1) * P], y[:, b, nt * P:(nt + 1) * P], ident)
                mm.then_inc(y_turned, 1)

            for i in range(8):
                channels_by_token(i, wk2, ctx_t, i // 2, i % 2)
                if i < 4:
                    for u in range(4 * i, 4 * i + 4):
                        project_out(2 * NKV, u, 1)
                    turn_y(i)
                elif i < 6:
                    turn_y(2 * i - 4)
                    turn_y(2 * i - 3)
                else:
                    turn_x(0, 2 * i - 12)
                    turn_x(0, 2 * i - 11)

            pe.wait_ge(q2_in, 16)
            pe.wait_ge(x_t_ready, BPH)
            for i in range(4):
                turn_x(0, BPH + i)
                channels_by_token(8 + i, wq2, x2_t, i, 0)

            def scores2(b):
                wait(pe, scores2_copied, b - 1)
                q = slice((b % BPH) * P, (b % BPH + 1) * P)
                for n in range(KC):
                    mm = nc.tensor.matmul(banks[4 * (b % 2) + n].rearrange("p (i q) -> p i q", q=P),
                                          k2_t[:, n, b * P:(b + 1) * P], q2_heads[:, n, :, q], start=True, stop=True)
                mm.then_inc(scored2, 1)

            pe.wait_ge(proj2_copied, 12)
            pe.wait_ge(x_t_ready, NB)
            for b in range(BPH):
                scores2(b)
            pe.wait_ge(scores2_copied, BPH - 1)
            for i in range(4):
                channels_by_token(12 + i, wq2, x2_t, i, 1)
            pe.wait_ge(proj2_copied, 16)
            for b in range(BPH, NB):
                scores2(b)

            pe.wait_ge(ones_ready, 2)
            pe.wait_ge(params_in, 64)
            pe.wait_ge(v2_in, 16)
            pe.wait_ge(scores2_copied, NB - 1)

            def values(b):
                i = 16 + b
                wait(pe, proj2_copied, i - 2)
                nc.tensor.matmul(banks[i % 3], ones[0:1, :], bias_v[:, :], start=True, stop=False)
                for g in range(KC):
                    mm = nc.tensor.matmul(banks[i % 3], ctx_t[:, g, b * P:(b + 1) * P], wv2[:, g, :],
                                          start=False, stop=(g == KC - 1))
                mm.then_inc(proj2_done, 1)

            def sum_exps(b):
                pe.wait_ge(exp2_done, b + 1)
                for i in range(4):
                    mm = nc.tensor.matmul(banks[7], ident, xs[:, SLOT[b], i * 512:(i + 1) * 512],
                                          start=(b == 0 and i == 0), stop=(b == PE_SUMS - 1 and i == 3))
                if b == PE_SUMS - 1:
                    mm.then_inc(part_summed, 1)

            for b in range(NB):
                values(b)
                if 0 <= b - 3 < PE_SUMS:
                    sum_exps(b - 3)

            pe.wait_ge(sum2_folded, 1)

            def attend(b):
                pe.wait_ge(weights2_ready, b + 1)
                pe.wait_ge(proj2_copied, 16 + b + 1)
                wait(pe, att_copied, b - 1)
                for n in range(KC):
                    for i in range(4):
                        h = 4 * n + i
                        mm = nc.tensor.matmul(att_bank(b)[32 * i:32 * i + 32, n * P:(n + 1) * P], v2[:, b, h * XD:(h + 1) * XD],
                                              xs[:, SLOT[b], h * P:(h + 1) * P], start=True, stop=True)
                mm.then_inc(pv2_done, 1)

            def turn_att(b):
                pe.wait_ge(att_copied, b + 1)
                wait(pe, attended2, b)
                for n in range(KC):
                    mm = nc.tensor.transpose(banks[7][:, n * P:(n + 1) * P], att_t[:, b % 2, n * P:(n + 1) * P], ident)
                mm.then_inc(att_turned, 1)

            def gate_and_lora(b):
                wait(pe, x_t_ready, NB + b + 1)
                for g in range(KC):
                    mm = nc.tensor.matmul(banks[b // 3][:, (b % 3) * (GH + ER):(b % 3 + 1) * (GH + ER)],
                                          x3_t[:, g, b * P:(b + 1) * P], w_ga[:, g, :], start=(g == 0), stop=(g == KC - 1))
                mm.then_inc(hidden_done, 1)

            def main(b, with_lora=False):
                wait(pe, x_t_ready, NB + b + 1)
                wait(pe, main_added, b - 1)
                for g in range(KC):
                    mm = nc.tensor.matmul(banks[3 + b % 2], x3_t[:, g, b * P:(b + 1) * P], w_main[:, g, :],
                                          start=(g == 0), stop=(g == KC - 1 and not with_lora))
                if not with_lora:
                    mm.then_inc(main_done, 1)

            def add_lora(b):
                pe.wait_ge(tmp_t_ready, b // 4 + 1)
                nc.tensor.matmul(banks[3 + b % 2], tmp_t[:, b * P:(b + 1) * P], w_b[:, :],
                                 start=False, stop=True).then_inc(main_done, 1)

            attend(0)
            attend(1)
            turn_att(0)
            attend(2)
            turn_att(1)
            attend(3)
            turn_att(2)
            attend(4)
            turn_x(1, 0)
            turn_att(3)
            turn_x(1, 1)
            pe.wait_ge(experts_in, 48)
            gate_and_lora(0)
            attend(5)
            turn_att(4)
            gate_and_lora(1)
            attend(6)
            turn_x(1, 2)
            turn_att(5)
            turn_x(1, 3)
            gate_and_lora(2)
            attend(7)
            turn_att(6)
            gate_and_lora(3)
            turn_att(7)
            turn_x(1, 4)
            turn_x(1, 5)
            gate_and_lora(4)
            gate_and_lora(5)
            turn_x(1, 6)
            turn_x(1, 7)
            gate_and_lora(6)
            gate_and_lora(7)
            main(0)
            main(1)
            pe.wait_ge(hid_ready, 1)
            pe.wait_ge(attended2, NB)
            for b in range(NB):
                mm = nc.tensor.transpose(banks[6 + b // 4][0:GH, (b % 4) * P:(b % 4 + 1) * P], hid[:, b, :], ident)
            mm.then_inc(hid_turned, 1)
            main(2)
            for b in range(NB):
                if b % 4 == 0:
                    pe.wait_ge(hid_t_ready, b // 4 + 1)
                mm = nc.tensor.matmul(banks[5][:, b * E:(b + 1) * E], hid_t[0:GH, b * P:(b + 1) * P], gw2_t[:, :],
                                      start=True, stop=True)
            mm.then_inc(gates_done, 1)
            main(3)
            pe.wait_ge(onehot_ready, 2)
            for b in range(NB):
                mm = nc.tensor.matmul(banks[5][:, 64:64 + 2 * E], ones[:, :], onehot[:, b, :], start=(b == 0), stop=(b == NB - 1))
            mm.then_inc(counted, 1)
            main(4)
            main(5, with_lora=True)
            pe.wait_ge(tmp_ready, 3)
            for b in range(NB):
                mm = nc.tensor.transpose(banks[6 + b // 4][:, (b % 4) * P:(b % 4 + 1) * P], tmp[:, b, :], ident)
            mm.then_inc(tmp_turned, 1)

            def lora(b):
                pe.wait_ge(tmp_t_ready, b // 4 + 1)
                wait(pe, lora_added, b - 2)
                nc.tensor.matmul(banks[b % 3], tmp_t[:, b * P:(b + 1) * P], w_b[:, :],
                                 start=True, stop=True).then_inc(lora_done, 1)

            lora(0)
            lora(1)
            add_lora(5)
            main(6, with_lora=True)
            add_lora(6)
            lora(2)
            lora(3)
            main(7, with_lora=True)
            lora(4)
            add_lora(7)


def constants():
    d = np.arange(P)
    inv = (np.float32(1.0) / np.float32(10000.0) ** (np.arange(0, P, 2, dtype=np.float32) / np.float32(P))).astype(np.float32)
    freqs = np.arange(P, dtype=np.float32)[:, None] * inv
    emb = np.concatenate([freqs, freqs], axis=-1).astype(np.float32)
    sign = np.where(d < P // 2, -1.0, 1.0).astype(np.float32)[:, None]
    mask = np.where(d[None, :] <= d[:, None], 0.0, NEG).astype(np.float32)
    return np.ascontiguousarray(np.stack([np.eye(P, dtype=np.float32), mask, np.cos(emb).T, np.sin(emb).T * sign], axis=1)).astype(np.float32)


def lay_out(i):
    i = {k: np.asarray(v) for k, v in i.items()}

    def by_chunk(w):
        return w.reshape(-1, P, w.shape[-1]).transpose(1, 0, 2)

    def qkv(q, k, v, rows):
        q = q.reshape(rows, NKV, QPK, P).transpose(1, 2, 0, 3)
        k = k.reshape(rows, NKV, 1, P).transpose(1, 2, 0, 3)
        v = v.reshape(rows, NKV, 1, P).transpose(1, 2, 0, 3)
        return np.concatenate([k, v, q], axis=1)

    a = {}
    tokens = i["x"].reshape(T, D)
    a["x_t"] = by_chunk(tokens.T)
    a["x"] = tokens.T.reshape(KC, P, NB, P).transpose(1, 2, 0, 3).reshape(P, NB, D)
    w = qkv(i["L0_attn_qw_q"], i["L0_attn_qw_k"], i["L0_attn_qw_v"], D)
    a["qkv"] = w.reshape(NKV, NT, KC, P, P).transpose(0, 3, 1, 2, 4)
    s = qkv(i["L0_attn_scales_q"], i["L0_attn_scales_k"], i["L0_attn_scales_v"], KC)
    a["qkv_scales"] = s.transpose(3, 0, 1, 2).reshape(P, NKV * NT * KC)
    a["o"] = i["L0_attn_qw_o"].reshape(NKV, QPK, P, D).transpose(0, 2, 1, 3)
    a["o_scales"] = i["L0_attn_scales_o"].reshape(NKV * QPK * KC, P).T
    a["consts"] = constants()
    a["wq2"] = by_chunk(i["L0_xattn_Wq"].T)
    a["wk2"] = by_chunk(i["L0_xattn_Wk"].T)
    a["wv2"] = by_chunk(i["L0_xattn_Wv"].T)
    a["ctx_t"] = by_chunk(i["ctx_4096"].reshape(T, D).T)
    a["bias_qk"] = np.concatenate([i["L0_xattn_bq"].reshape(KC, P).T, i["L0_xattn_bk"].reshape(KC, P).T], axis=1)
    a["bias_v"] = i["L0_xattn_bv"].reshape(1, D)
    a["w_main"] = by_chunk(i["L0_ffn_weight"].T)
    a["w_ga"] = by_chunk(np.concatenate([i["L0_ffn_gw1"].T, i["L0_ffn_lora_A"].transpose(1, 0, 2).reshape(D, ER)], axis=1))
    a["w_b"] = i["L0_ffn_lora_B"].reshape(ER, D)
    a["gw2_t"] = i["L0_ffn_gw2"].T
    a["params"] = np.concatenate([i["L0_ffn_gb1"], i["L0_ffn_ln_gamma"], i["L0_ffn_ln_beta"], i["L0_ffn_gb2"],
                                  np.arange(E, dtype=np.float32)])
    return {k: np.ascontiguousarray(v) for k, v in a.items()}


def kernel(**inputs):
    import concourse.bacc as _bacc
    from concourse.bass_utils import run_bass_kernel_spmd as _run

    nc = _bacc.Bacc("TRN2", target_bir_lowering=False, num_devices=1)
    arrays = {f"in_{k}": v for k, v in lay_out(inputs).items()}
    t = {k[3:]: nc.dram_tensor(k, v.shape, mybir.dt.from_np(v.dtype), kind="ExternalInput").ap() for k, v in arrays.items()}
    out = nc.dram_tensor("out", (P, NB, D), F32, kind="ExternalOutput").ap()
    build(nc, t, out)
    r = _run(nc, [arrays], core_ids=[0])
    return np.ascontiguousarray(r.results[0]["out"].transpose(1, 0, 2))
```
